# Optimizing a Trainium2 kernel written in Bass

```python
import numpy as np
import jax
import jax.numpy as jnp

def _softmax(x, axis=-1):
    return jax.nn.softmax(x, axis=axis)

def _gelu(x):
    return jax.nn.gelu(x, approximate=True)

def _silu(x):
    return jax.nn.silu(x)

def _sigmoid(x):
    return jax.nn.sigmoid(x)

def _layernorm(x, axis=-1, eps=1e-05):
    m = jnp.mean(x, axis=axis, keepdims=True)
    v = jnp.var(x, axis=axis, keepdims=True)
    return (x - m) / jnp.sqrt(v + eps)

def _scatter_add(tgt, idx, src, axis=0):
    return tgt.at[idx].add(src)

def _segment_sum(src, seg, n):
    return jax.ops.segment_sum(src, seg, n)
kernel_name = 'mk_vit_tower_d1_tok_img768_r4_5b4ac8'

def setup_inputs(seed: int=0):
    np.random.seed(seed)
    _w = jnp.asarray

    def _rec_inputs():
        import jax
        import jax.numpy as jnp
        _rk = jax.random.key(seed)
        x = -0.000356955 + 1 * jax.random.normal(jax.random.fold_in(_rk, 1), (64, 3, 224, 224), jnp.float32)
        return x
    x = _rec_inputs()

    def _L0_tok_setup():
        import jax, jax.numpy as jnp
        import numpy as np
        C, H, W = (3, 224, 224)
        P = 14
        PS = H // P
        PATCH_DIM = C * PS * PS
        HIDDEN = 192

        def patchify(images):
            n = images.shape[0]
            x = images.reshape(n, C, P, PS, P, PS)
            x = x.transpose(0, 2, 4, 1, 3, 5)
            return x.reshape(n, P * P, PATCH_DIM)
        key = jax.random.key(seed)
        k1, k2, k3 = jax.random.split(key, 3)
        images = jax.random.normal(k1, (128, C, H, W), dtype=jnp.float32)
        bound = 1.0 / np.sqrt(PATCH_DIM)
        W_lin = jax.random.uniform(k2, (HIDDEN, PATCH_DIM), minval=-bound, maxval=bound, dtype=jnp.float32)
        b_lin = jax.random.uniform(k3, (HIDDEN,), minval=-bound, maxval=bound, dtype=jnp.float32)
        cls_token = jnp.ones((1, HIDDEN), dtype=jnp.float32)
        return {'images': images, 'W_lin': W_lin, 'b_lin': b_lin, 'cls_token': cls_token}
    _L0_tok_all = _L0_tok_setup()
    _L0_tok_in = {k: v for k, v in _L0_tok_all.items() if k in ('W_lin', 'b_lin', 'cls_token')}
    del _L0_tok_all

    def _L0_attn_setup():
        import jax, jax.numpy as jnp
        import numpy as np
        import math
        B, S, D = (4, 1024, 192)
        key = jax.random.key(seed)
        ks = jax.random.split(key, 7)
        sc = 0.02
        return {'x': jax.random.normal(ks[0], (B, S, D), dtype=jnp.float32), 'Wq': jax.random.normal(ks[1], (D, D), dtype=jnp.float32) * sc, 'bq': jax.random.normal(ks[2], (D,), dtype=jnp.float32) * sc, 'Wk': jax.random.normal(ks[3], (D, D), dtype=jnp.float32) * sc, 'bk': jax.random.normal(ks[4], (D,), dtype=jnp.float32) * sc, 'Wv': jax.random.normal(ks[5], (D, D), dtype=jnp.float32) * sc, 'bv': jax.random.normal(ks[6], (D,), dtype=jnp.float32) * sc}
    _L0_attn_all = _L0_attn_setup()
    _L0_attn_in = {k: v for k, v in _L0_attn_all.items() if k in ('Wq', 'bq', 'Wk', 'bk', 'Wv', 'bv')}
    del _L0_attn_all

    def _L0_ffn_setup():
        import jax, jax.numpy as jnp
        import numpy as np
        E = 16
        D = 192
        K = D // 2
        SI = 2 * D
        B, N = (8, 1024)

        def _moe_mlp(x, gw, uw, dw):
            return jax.nn.silu(x @ gw) * (x @ uw) @ dw
        key = jax.random.key(seed)
        ks = jax.random.split(key, 20)
        s = lambda fan_in: 1.0 / np.sqrt(fan_in)
        inp = {}
        inp['hidden_states'] = jax.random.normal(ks[0], (B, N, D), jnp.float32)
        inp['posembed'] = jax.random.normal(ks[1], (E, D), jnp.float32)
        inp['pos_w'] = jax.random.uniform(ks[2], (D, D), jnp.float32, -s(D), s(D))
        inp['pos_b'] = jax.random.uniform(ks[3], (D,), jnp.float32, -s(D), s(D))
        inp['gate_w'] = jax.random.uniform(ks[4], (D, D), jnp.float32, -s(D), s(D))
        inp['gate_b'] = jax.random.uniform(ks[5], (D,), jnp.float32, -s(D), s(D))
        inp['eg_w'] = jax.random.uniform(ks[6], (E, K, D), jnp.float32, -s(K), s(K))
        inp['eu_w'] = jax.random.uniform(ks[7], (E, K, D), jnp.float32, -s(K), s(K))
        inp['ed_w'] = jax.random.uniform(ks[8], (E, D, D), jnp.float32, -s(D), s(D))
        inp['sg_w'] = jax.random.uniform(ks[9], (D, SI), jnp.float32, -s(D), s(D))
        inp['su_w'] = jax.random.uniform(ks[10], (D, SI), jnp.float32, -s(D), s(D))
        inp['sd_w'] = jax.random.uniform(ks[11], (SI, D), jnp.float32, -s(SI), s(SI))
        inp['ln_g'] = jnp.ones((D,), jnp.float32)
        inp['ln_b'] = jnp.zeros((D,), jnp.float32)
        inp['m1_w'] = jax.random.uniform(ks[12], (D, D), jnp.float32, -s(D), s(D))
        inp['m1_b'] = jax.random.uniform(ks[13], (D,), jnp.float32, -s(D), s(D))
        inp['m2_w'] = jax.random.uniform(ks[14], (D, D), jnp.float32, -s(D), s(D))
        inp['m2_b'] = jax.random.uniform(ks[15], (D,), jnp.float32, -s(D), s(D))
        return inp
    _L0_ffn_all = _L0_ffn_setup()
    _L0_ffn_in = {k: v for k, v in _L0_ffn_all.items() if k in ('posembed', 'pos_w', 'pos_b', 'gate_w', 'gate_b', 'eg_w', 'eu_w', 'ed_w', 'sg_w', 'su_w', 'sd_w', 'ln_g', 'ln_b', 'm1_w', 'm1_b', 'm2_w', 'm2_b')}
    del _L0_ffn_all
    return {'x': x, 'L0_tok_W_lin': _L0_tok_in['W_lin'], 'L0_tok_b_lin': _L0_tok_in['b_lin'], 'L0_tok_cls_token': _L0_tok_in['cls_token'], 'L0_attn_Wq': _L0_attn_in['Wq'], 'L0_attn_bq': _L0_attn_in['bq'], 'L0_attn_Wk': _L0_attn_in['Wk'], 'L0_attn_bk': _L0_attn_in['bk'], 'L0_attn_Wv': _L0_attn_in['Wv'], 'L0_attn_bv': _L0_attn_in['bv'], 'L0_ffn_posembed': _L0_ffn_in['posembed'], 'L0_ffn_pos_w': _L0_ffn_in['pos_w'], 'L0_ffn_pos_b': _L0_ffn_in['pos_b'], 'L0_ffn_gate_w': _L0_ffn_in['gate_w'], 'L0_ffn_gate_b': _L0_ffn_in['gate_b'], 'L0_ffn_eg_w': _L0_ffn_in['eg_w'], 'L0_ffn_eu_w': _L0_ffn_in['eu_w'], 'L0_ffn_ed_w': _L0_ffn_in['ed_w'], 'L0_ffn_sg_w': _L0_ffn_in['sg_w'], 'L0_ffn_su_w': _L0_ffn_in['su_w'], 'L0_ffn_sd_w': _L0_ffn_in['sd_w'], 'L0_ffn_ln_g': _L0_ffn_in['ln_g'], 'L0_ffn_ln_b': _L0_ffn_in['ln_b'], 'L0_ffn_m1_w': _L0_ffn_in['m1_w'], 'L0_ffn_m1_b': _L0_ffn_in['m1_b'], 'L0_ffn_m2_w': _L0_ffn_in['m2_w'], 'L0_ffn_m2_b': _L0_ffn_in['m2_b']}

def reference(x, L0_tok_W_lin, L0_tok_b_lin, L0_tok_cls_token, L0_attn_Wq, L0_attn_bq, L0_attn_Wk, L0_attn_bk, L0_attn_Wv, L0_attn_bv, L0_ffn_posembed, L0_ffn_pos_w, L0_ffn_pos_b, L0_ffn_gate_w, L0_ffn_gate_b, L0_ffn_eg_w, L0_ffn_eu_w, L0_ffn_ed_w, L0_ffn_sg_w, L0_ffn_su_w, L0_ffn_sd_w, L0_ffn_ln_g, L0_ffn_ln_b, L0_ffn_m1_w, L0_ffn_m1_b, L0_ffn_m2_w, L0_ffn_m2_b):
    import jax
    import jax.numpy as jnp

    def _L0_tok_ref(images, W_lin, b_lin, cls_token):
        import jax, jax.numpy as jnp
        import numpy as np
        C, H, W = (3, 224, 224)
        P = 14
        PS = H // P
        PATCH_DIM = C * PS * PS
        HIDDEN = 192

        def patchify(images):
            n = images.shape[0]
            x = images.reshape(n, C, P, PS, P, PS)
            x = x.transpose(0, 2, 4, 1, 3, 5)
            return x.reshape(n, P * P, PATCH_DIM)
        patches = patchify(images)
        hidden = jnp.einsum('npd,hd->nph', patches, W_lin) + b_lin
        n = images.shape[0]
        cls = jnp.broadcast_to(cls_token[None], (n, 1, HIDDEN))
        return jnp.concatenate([cls, hidden], axis=1)

    def _L0_attn_ref(x, Wq, bq, Wk, bk, Wv, bv):
        import jax, jax.numpy as jnp
        import numpy as np
        import math
        B, S, D = (4, 1024, 192)
        q = jnp.einsum('bsd,ed->bse', x, Wq) + bq
        k = jnp.einsum('bsd,ed->bse', x, Wk) + bk
        v = jnp.einsum('bsd,ed->bse', x, Wv) + bv
        scale = 1.0 / math.sqrt(x.shape[-1])
        scores = jnp.einsum('bsd,btd->bst', q, k) * scale
        return jnp.einsum('bst,btd->bsd', scores, v)

    def _L0_ffn_ref(hidden_states, posembed, pos_w, pos_b, gate_w, gate_b, eg_w, eu_w, ed_w, sg_w, su_w, sd_w, ln_g, ln_b, m1_w, m1_b, m2_w, m2_b):
        import jax, jax.numpy as jnp
        import numpy as np
        E = 16
        D = 192
        K = D // 2
        SI = 2 * D
        B, N = (8, 1024)

        def _moe_mlp(x, gw, uw, dw):
            return jax.nn.silu(x @ gw) * (x @ uw) @ dw
        pe = jax.nn.softmax(posembed @ pos_w + pos_b, axis=-1)
        y = _moe_mlp(hidden_states, sg_w, su_w, sd_w)
        for i in range(E):
            gate_feature = hidden_states * pe[i] @ gate_w + gate_b
            gate_weight, gate_idx = jax.lax.top_k(gate_feature, K)
            gate_weight = jax.nn.softmax(gate_weight, axis=-1)
            gathered = jnp.take_along_axis(hidden_states, gate_idx, axis=-1)
            y = y + _moe_mlp(gathered * gate_weight, eg_w[i], eu_w[i], ed_w[i])
        mu = jnp.mean(y, axis=-1, keepdims=True)
        var = jnp.mean(jnp.square(y - mu), axis=-1, keepdims=True)
        yn = (y - mu) * jax.lax.rsqrt(var + 1e-06) * ln_g + ln_b
        return jax.nn.silu(yn @ m1_w + m1_b) @ m2_w + m2_b
    h = _L0_tok_ref(x, L0_tok_W_lin, L0_tok_b_lin, L0_tok_cls_token)
    h = h + _L0_attn_ref(_layernorm(h, axis=-1), L0_attn_Wq, L0_attn_bq, L0_attn_Wk, L0_attn_bk, L0_attn_Wv, L0_attn_bv)
    h = h + _L0_ffn_ref(_layernorm(h, axis=-1), L0_ffn_posembed, L0_ffn_pos_w, L0_ffn_pos_b, L0_ffn_gate_w, L0_ffn_gate_b, L0_ffn_eg_w, L0_ffn_eu_w, L0_ffn_ed_w, L0_ffn_sg_w, L0_ffn_su_w, L0_ffn_sd_w, L0_ffn_ln_g, L0_ffn_ln_b, L0_ffn_m1_w, L0_ffn_m1_b, L0_ffn_m2_w, L0_ffn_m2_b)
    return h

_drawn_inputs = setup_inputs


def setup_inputs(seed=0):
    import zlib

    import numpy as np

    out = dict(_drawn_inputs(seed))
    spreads = {'L0_tok_cls_token': (1.0, 0.2), 'L0_ffn_ln_g': (1.0, 0.2), 'L0_ffn_ln_b': (0.0, 0.33)}
    factors = {'L0_ffn_posembed': 8.0,
     'L0_ffn_pos_w': 8.0,
     'L0_ffn_pos_b': 8.0,
     'L0_ffn_gate_w': 8.0,
     'L0_ffn_gate_b': 8.0,
     'L0_ffn_eg_w': 8.0,
     'L0_ffn_eu_w': 8.0,
     'L0_ffn_ed_w': 8.0,
     'L0_ffn_m1_b': 3.2}
    for name, (base, spread) in spreads.items():
        noise = np.random.default_rng([zlib.crc32(name.encode()), seed]).standard_normal(out[name].shape)
        drawn = base * np.exp(spread * noise) if base else spread * noise
        out[name] = jnp.asarray(drawn.astype(out[name].dtype))
    for name, factor in factors.items():
        out[name] = (out[name] * factor).astype(out[name].dtype)
    return out
```

```python
from contextlib import ExitStack

import concourse.bass as bass
from concourse import mybir

ALU = mybir.AluOpType
ACT = mybir.ActivationFunctionType
F32 = mybir.dt.float32
BF16 = mybir.dt.bfloat16
U16 = mybir.dt.uint16

IMAGES, SIDE, PATCH, CHANNELS = 64, 14, 16, 3
TOKENS = SIDE * SIDE + 1
PATCH_DIM = CHANNELS * PATCH * PATCH
PC = PATCH_DIM // 128
D = 192
HALF = D // 2
CHUNK = [99, 98]
E = 16
K = D // 2
SI = 2 * D
ROUNDS = K // 8
ROWS = IMAGES * TOKENS
TILES = -(-ROWS // 128)
PADDED = (TILES + 1) * 128
LO, HI = 16, D // 16
GROUP = 8
GROUPS = 128 // GROUP
WIDE = 512
PARTS = E * K // WIDE
UNITS = GROUPS * PARTS
RING = 3
SHARED = SI // D
BLOCKS = E + SHARED
GATES = E // 2
LOWEST = -3.0e38
SORT_INCS = 2 * 2 * ROUNDS * (E // 2)
PER_STEP = 4


def wait(engine, semaphore, value):
    if isinstance(value, int) and value <= 0:
        return
    engine.wait_ge(semaphore, value)


def phase_a(nc, t, h1_dram, x2_dram):
    with ExitStack() as ctx:
        def sb(name, shape, dt=F32):
            return ctx.enter_context(nc.sbuf_tensor(name, shape, dt))

        def sem(name):
            return ctx.enter_context(nc.semaphore(name))

        n_img = PER_STEP
        wlin = sb("wlin", [128, PC, D])
        base = sb("base", [CHUNK[0], 2, D])
        wq = sb("wq", [HALF, 2, D])
        bq = sb("bq", [HALF, 2])
        wkv = sb("wkv", [HALF + 1, 2, 2 * D])
        ident = sb("ident_a", [128, 128])
        eps = sb("eps_a", [128, 1])
        zeros = sb("zeros", [128, D])
        patches = [sb(f"patches{i}", [128, PC, TOKENS]) for i in range(n_img)]
        h0 = [sb(f"h0_{i}", [CHUNK[0], 2, D]) for i in range(n_img)]
        stats = [sb(f"stats{i}", [CHUNK[0], 2, 6]) for i in range(n_img)]
        mv = [sb(f"mv{i}", [CHUNK[0], 2, 2]) for i in range(n_img)]
        sd = [sb(f"sd{i}", [CHUNK[0], 2]) for i in range(n_img)]
        rstd = [sb(f"rstd{i}", [CHUNK[0], 2]) for i in range(n_img)]
        xn = [sb(f"xn{i}", [CHUNK[0], 2, D]) for i in range(n_img)]
        xnt = [sb(f"xnt{i}", [HALF + 1, 2, TOKENS]) for i in range(n_img)]
        qt = [sb(f"qt{i}", [HALF, 2, TOKENS]) for i in range(n_img)]
        kv = [sb(f"kv{i}", [CHUNK[0], 2, 2 * D]) for i in range(n_img)]
        kvm = [sb(f"kvm{i}", [HALF, 2, D]) for i in range(n_img)]
        h1 = [sb(f"h1_{i}", [CHUNK[0], 2, D]) for i in range(n_img)]
        x2 = [sb(f"x2_{i}", [CHUNK[0], 2, D]) for i in range(n_img)]
        pa = [ctx.enter_context(nc.psum_tensor(f"pa{i}", [128, WIDE], F32)) for i in range(n_img)]
        pb = [ctx.enter_context(nc.psum_tensor(f"pb{i}", [128, WIDE], F32)) for i in range(n_img)]

        s_w = sem("a_weights")
        s_zero = sem("a_zeros")
        s_eps = sem("a_eps")
        s_held = sem("a_vector_waits_passed")
        s_ones = sem("a_ones_row")
        s_in = [sem(f"a_patches_loaded{i}") for i in range(n_img)]
        s_emb = sem("a_embedded")
        s_h0 = sem("a_h0")
        s_st = sem("a_stats")
        s_mv = sem("a_moments")
        s_sd = sem("a_deviation")
        s_rs = sem("a_reciprocal")
        s_xn = sem("a_normed")
        s_xtp = sem("a_transposed")
        s_xt = sem("a_transpose_copied")
        s_q = sem("a_q_product")
        s_qt = sem("a_q_copied")
        s_kvp = sem("a_kv_product")
        s_kv = sem("a_kv_copied")
        s_mp = sem("a_memory_product")
        s_m = sem("a_memory_copied")
        s_op = sem("a_attended")
        s_h1 = sem("a_h1")
        s_st2 = sem("a_stats2")
        s_mv2 = sem("a_moments2")
        s_sd2 = sem("a_deviation2")
        s_rs2 = sem("a_reciprocal2")
        s_x2 = sem("a_normed2")
        s_out = sem("a_stored")
        N_W = 6 * 16

        def steps(engine, body):
            body(0)
            with engine.Fori(1, IMAGES // n_img) as it:
                body(it)

        with nc.Block() as block:
            @block.sync
            def _(sp):
                sp.dma_start(wlin[:], t["w_lin"].rearrange("(c p) n -> p c n", p=128)).then_inc(s_w, 16)
                sp.dma_start(base[:], t["base"].rearrange("c p n -> p c n")).then_inc(s_w, 16)
                sp.dma_start(wq[:], t["wq"].rearrange("(c p) n -> p c n", p=HALF)).then_inc(s_w, 16)
                sp.dma_start(bq[:], t["bq"]).then_inc(s_w, 16)
                sp.dma_start(wkv[:], t["wkv"].rearrange("c p n -> p c n")).then_inc(s_w, 16)
                sp.dma_start(ident[:], t["ident"]).then_inc(s_w, 16)

                def body(it):
                    for i in range(n_img):
                        wait(sp, s_emb, n_img * (it - 1) + i + 1)
                        sp.dma_start(patches[i][:], t["patches"][bass.ds(n_img * it + i, 1)]
                                     .rearrange("a p c n -> (a p) c n")).then_inc(s_in[i], 16)
                steps(sp, body)

            @block.gpsimd
            def _(pool):
                nc.gpsimd.memset(zeros[:], 0.0).then_inc(s_zero, 1)
                pool.wait_ge(s_zero, 1)
                for first in range(ROWS, PADDED, 64):
                    for dram in (h1_dram, x2_dram):
                        pool.dma_start(dram[first:first + 64], zeros[0:64, :]).then_inc(s_out, 16)

                def body(it):
                    for i in range(n_img):
                        pool.wait_ge(s_x2, n_img * it + i + 1)
                        row = TOKENS * (n_img * it + i)
                        for c, size in enumerate(CHUNK):
                            first = row + c * CHUNK[0]
                            pool.dma_start(h1_dram[bass.ds(first, size)], h1[i][0:size, c, :]).then_inc(s_out, 16)
                            pool.dma_start(x2_dram[bass.ds(first, size)], x2[i][0:size, c, :]).then_inc(s_out, 16)
                steps(pool, body)
                pool.wait_ge(s_out, 16 * (4 * IMAGES + 2 * (PADDED - ROWS) // 64))

            @block.tensor
            def _(pe):
                pe.wait_ge(s_w, N_W)

                def body(it):
                    def n(i):
                        return n_img * it + i + 1
                    for i in range(n_img):
                        wait(pe, s_qt, n(i) - n_img)
                        wait(pe, s_kv, 2 * (n(i) - n_img))
                        pe.wait_ge(s_in[i], 16 * (it + 1))
                        for c, size in enumerate(CHUNK):
                            for p in range(PC):
                                mm = nc.tensor.matmul(pa[i][0:size, c * D:(c + 1) * D],
                                                      patches[i][:, p, c * CHUNK[0]:c * CHUNK[0] + size],
                                                      wlin[:, p, :], start=p == 0, stop=p == PC - 1)
                        mm.then_inc(s_emb, 1)
                    for i in range(n_img):
                        wait(pe, s_h1, n(i) - n_img)
                        pe.wait_ge(s_xn, n(i))
                        for f in range(2):
                            for c, size in enumerate(CHUNK):
                                at = f * TOKENS + c * CHUNK[0]
                                mm = nc.tensor.transpose(pb[i][0:HALF, at:at + size],
                                                         xn[i][0:size, c, f * HALF:(f + 1) * HALF],
                                                         ident[0:size, 0:size])
                        mm.then_inc(s_xtp, 1)
                    for i in range(n_img):
                        pe.wait_ge(s_h0, n(i))
                        pe.wait_ge(s_ones, 1)
                        pe.wait_ge(s_xt, n(i))
                        for e in range(2):
                            for f in range(2):
                                mm = nc.tensor.matmul(pa[i][0:HALF, e * TOKENS:(e + 1) * TOKENS],
                                                      wq[:, f, e * HALF:(e + 1) * HALF], xnt[i][0:HALF, f, :],
                                                      start=f == 0, stop=f == 1)
                        mm.then_inc(s_q, 1)
                    for i in range(n_img):
                        for c, size in enumerate(CHUNK):
                            if c:
                                pe.wait_ge(s_qt, n(i))
                            out = (pb, pa)[c][i]
                            for f in range(2):
                                mm = nc.tensor.matmul(out[0:size, 0:2 * D],
                                                      xnt[i][0:HALF + f, f, c * CHUNK[0]:c * CHUNK[0] + size],
                                                      wkv[0:HALF + f, f, :], start=f == 0, stop=f == 1)
                            mm.then_inc(s_kvp, 1)
                    for i in range(n_img):
                        pe.wait_ge(s_kv, 2 * n(i))
                        for f in range(2):
                            for c, size in enumerate(CHUNK):
                                mm = nc.tensor.matmul(pb[i][0:HALF, f * D:(f + 1) * D],
                                                      kv[i][0:size, c, f * HALF:(f + 1) * HALF],
                                                      kv[i][0:size, c, D:2 * D], start=c == 0, stop=c == 1)
                        mm.then_inc(s_mp, 1)
                    for i in range(n_img):
                        pe.wait_ge(s_m, n(i))
                        for c, size in enumerate(CHUNK):
                            for f in range(2):
                                mm = nc.tensor.matmul(pb[i][0:size, c * D:(c + 1) * D],
                                                      qt[i][:, f, c * CHUNK[0]:c * CHUNK[0] + size],
                                                      kvm[i][:, f, :], start=f == 0, stop=f == 1)
                        mm.then_inc(s_op, 1)
                steps(pe, body)

            @block.vector
            def _(dve):
                nc.vector.memset(eps[:], 1e-5).then_inc(s_eps, 1)
                for i in range(n_img):
                    op = nc.vector.memset(xnt[i][HALF:HALF + 1, :, :], 1.0)
                op.then_inc(s_ones, 1)
                dve.wait_ge(s_w, N_W)

                def norm(it, src, dst, s_src, s_stat, s_mom, s_dev, s_rec, s_dst):
                    def n(i):
                        return n_img * it + i + 1
                    for i in range(n_img):
                        dve.wait_ge(s_src, n(i))
                        wait(dve, s_dst, n(i) - n_img)
                        for c, size in enumerate(CHUNK):
                            op = nc.vector.bn_stats(stats[i][0:size, c, :], src[i][0:size, c, :])
                        op.then_inc(s_stat, 1)
                    for i in range(n_img):
                        dve.wait_ge(s_stat, n(i))
                        dve.sem_inc(s_held, 1)
                        for c, size in enumerate(CHUNK):
                            op = nc.vector.bn_aggr(mv[i][0:size, c, :], stats[i][0:size, c, :])
                        op.then_inc(s_mom, 1)
                    for i in range(n_img):
                        dve.wait_ge(s_dev, n(i))
                        for c, size in enumerate(CHUNK):
                            op = nc.vector.reciprocal(rstd[i][0:size, c:c + 1], sd[i][0:size, c:c + 1])
                        op.then_inc(s_rec, 1)
                    for i in range(n_img):
                        dve.wait_ge(s_rec, n(i))
                        for c, size in enumerate(CHUNK):
                            op = nc.vector.tensor_scalar(dst[i][0:size, c, :], src[i][0:size, c, :],
                                                         mv[i][0:size, c, 0:1], rstd[i][0:size, c:c + 1],
                                                         ALU.subtract, ALU.mult)
                        op.then_inc(s_dst, 1)

                def body(it):
                    def n(i):
                        return n_img * it + i + 1
                    for i in range(n_img):
                        dve.wait_ge(s_emb, n(i))
                        for c, size in enumerate(CHUNK):
                            op = nc.vector.tensor_tensor(h0[i][0:size, c, :], pa[i][0:size, c * D:(c + 1) * D],
                                                         base[0:size, c, :], ALU.add)
                        op.then_inc(s_h0, 1)
                    norm(it, h0, xn, s_h0, s_st, s_mv, s_sd, s_rs, s_xn)
                    for i in range(n_img):
                        for c, size in enumerate(CHUNK):
                            dve.wait_ge(s_kvp, 2 * (n(i) - 1) + c + 1)
                            nc.vector.tensor_copy(kv[i][0:size, c, :], (pb, pa)[c][i][0:size, 0:2 * D])\
                                .then_inc(s_kv, 1)
                    for i in range(n_img):
                        if i == 0 and not isinstance(it, int):
                            dve.wait_ge(s_out, 16 * (4 * n_img * it + 2 * (PADDED - ROWS) // 64))
                        dve.wait_ge(s_op, n(i))
                        for c, size in enumerate(CHUNK):
                            op = nc.vector.tensor_tensor(h1[i][0:size, c, :], pb[i][0:size, c * D:(c + 1) * D],
                                                         h0[i][0:size, c, :], ALU.add)
                        op.then_inc(s_h1, 1)
                    norm(it, h1, x2, s_h1, s_st2, s_mv2, s_sd2, s_rs2, s_x2)
                steps(dve, body)

            @block.scalar
            def _(act):
                act.wait_ge(s_eps, 1)
                act.wait_ge(s_w, N_W)

                def body(it):
                    def n(i):
                        return n_img * it + i + 1
                    for i in range(n_img):
                        act.wait_ge(s_mv, n(i))
                        for c, size in enumerate(CHUNK):
                            op = nc.scalar.activation(sd[i][0:size, c:c + 1], mv[i][0:size, c, 1:2], ACT.Sqrt,
                                                      bias=eps[0:size, :])
                        op.then_inc(s_sd, 1)
                    for i in range(n_img):
                        act.wait_ge(s_xtp, n(i))
                        nc.scalar.activation(xnt[i][0:HALF, :, :].rearrange("p a b -> p (a b)"),
                                             pb[i][0:HALF, 0:2 * TOKENS], ACT.Copy).then_inc(s_xt, 1)
                    for i in range(n_img):
                        act.wait_ge(s_q, n(i))
                        for e in range(2):
                            op = nc.scalar.activation(qt[i][:, e, :], pa[i][0:HALF, e * TOKENS:(e + 1) * TOKENS],
                                                      ACT.Identity, bias=bq[:, e:e + 1])
                        op.then_inc(s_qt, 1)
                    for i in range(n_img):
                        act.wait_ge(s_mp, n(i))
                        nc.scalar.activation(kvm[i][:].rearrange("p a b -> p (a b)"), pb[i][0:HALF, 0:2 * D],
                                             ACT.Copy, scale=float(D) ** -0.5).then_inc(s_m, 1)
                    for i in range(n_img):
                        act.wait_ge(s_mv2, n(i))
                        for c, size in enumerate(CHUNK):
                            op = nc.scalar.activation(sd[i][0:size, c:c + 1], mv[i][0:size, c, 1:2], ACT.Sqrt,
                                                      bias=eps[0:size, :])
                        op.then_inc(s_sd2, 1)
                steps(act, body)


def phase_b(nc, t, h1_dram, x2_dram, out):
    with ExitStack() as ctx:
        def sb(name, shape, dt=F32):
            return ctx.enter_context(nc.sbuf_tensor(name, shape, dt))

        def sem(name):
            return ctx.enter_context(nc.semaphore(name))

        gatew = sb("gatew", [HALF + 1, 2, E * D])
        w_gu = sb("w_gu", [K, E, 2 * D])
        w_dn = sb("w_dn", [HALF, E, 2, D])
        ws_gu = sb("ws_gu", [HALF, 2, 2 * SI])
        ws_dn = sb("ws_dn", [HALF, SHARED, 2, D])
        m1 = sb("m1", [HALF, 2, D])
        m2 = sb("m2", [HALF, 2, D])
        m2b = sb("m2b", [1, D])
        cols = sb("cols", [HALF, 6])
        ident = sb("ident_b", [128, 128])
        pick_hi = sb("pick_hi", [128, GROUPS, GROUP * HI], BF16)
        pick_lo = sb("pick_lo", [128, GROUPS, GROUP * LO], BF16)
        gather = sb("gather", [GROUP * LO, 2 * 128 - GROUP])
        own_hi = sb("own_hi", [GROUP * HI, 1])
        own_lo = sb("own_lo", [GROUP * LO, 1])
        ones = sb("ones", [1, 128])
        eps = sb("eps_b", [128, 1])
        xin = sb("xin", [128, D])
        xsh = sb("xsh", [128, D])
        h1t = sb("h1t", [128, D])
        xt = sb("xt", [HALF + 1, 2, 128])
        xst = sb("xst", [HALF, 2, 128])
        g = [sb(f"g{b}", [128, E, D]) for b in range(2)]
        w = [sb(f"w{b}", [128, E, K]) for b in range(2)]
        idx = sb("idx", [128, E, K], U16)
        hi = sb("hi", [128, E * K], BF16)
        lo = sb("lo", [128, E * K], BF16)
        nmax = sb("nmax", [128, E])
        total = sb("total", [128, E])
        rtotal = sb("rtotal", [128, E])
        xbd = sb("xbd", [GROUP * HI, GROUPS, GROUP, LO])
        hi_s = [sb(f"hi_s{r}", [GROUP * HI, WIDE], BF16) for r in range(RING)]
        lo_s = [sb(f"lo_s{r}", [GROUP * LO, WIDE], BF16) for r in range(RING)]
        hot = [sb(f"hot{r}", [GROUP * HI, WIDE]) for r in range(RING)]
        cand = [sb(f"cand{r}", [GROUP * LO, WIDE]) for r in range(RING)]
        kept = [sb(f"kept{r}", [GROUP * LO, WIDE]) for r in range(RING)]
        gwt = [sb(f"gwt{b}", [K, 4, 128]) for b in range(2)]
        silu = [sb(f"silu{b}", [HALF, 2 * 128]) for b in range(2)]
        act_s = [sb(f"act{b}", [HALF, 2 * 128]) for b in range(2)]
        carrier = sb("carrier", [128, 1])
        stats = sb("stats_b", [128, 6])
        mv = sb("mv_b", [128, 2])
        sd = sb("sd_b", [128, 1])
        rstd = sb("rstd_b", [128, 1])
        yn = sb("yn", [128, D])
        ynt = sb("ynt", [HALF, 2, 128])
        mid = sb("mid", [HALF, 2, 128])
        res = sb("res", [128, D])

        bank = [ctx.enter_context(nc.psum_tensor(f"bank{i}", [128, WIDE], F32)) for i in range(8)]
        acc = bank[0:3]
        p_hi, p_lo, p_cand, p_misc = bank[3], bank[4], bank[5:7], bank[7]
        p_h, p_t, p_y = bank[3:5], bank[5], bank[6]

        s_w = sem("b_weights")
        s_const = sem("b_constants")
        s_held = sem("b_pool_waits_passed")
        s_held_v = sem("b_vector_waits_passed")
        s_pe = sem("b_posembed")
        s_pet = sem("b_posembed_steps")
        s_gw0 = sem("b_gate_weights")
        s_xin = sem("b_x_loaded")
        s_xsh = sem("b_shared_x_loaded")
        s_h1 = sem("b_h1_loaded")
        s_bd = sem("b_block_diagonal_loaded")
        s_xtp = sem("b_x_transposed")
        s_xt = sem("b_xt_copied")
        s_gp = sem("b_gate_product")
        s_g = sem("b_gate_copied")
        s_sort = sem("b_sort_chain")
        s_idx = sem("b_index_parts")
        s_cast = sem("b_index_cast")
        s_nmax = sem("b_negative_max")
        s_exp = sem("b_exponentials")
        s_rt = sem("b_reciprocal_totals")
        s_wt = sem("b_gate_softmax")
        s_hp = sem("b_hi_broadcast")
        s_lp = sem("b_lo_broadcast")
        s_hs = sem("b_hi_copied")
        s_ls = sem("b_lo_copied")
        s_hot = sem("b_one_hot")
        s_mask = sem("b_mask")
        s_cp = sem("b_candidates")
        s_cs = sem("b_candidates_copied")
        s_kept = sem("b_kept")
        s_acc = sem("b_accumulated")
        s_gx = sem("b_gathered_weighted")
        s_tp = sem("b_gathered_transposed")
        s_ts = sem("b_gathered_transpose_copied")
        s_xsp = sem("b_shared_x_transposed")
        s_xss = sem("b_shared_x_copied")
        s_h = sem("b_hidden")
        s_si = sem("b_silu")
        s_a = sem("b_activated")
        s_dn = sem("b_down")
        s_st = sem("b_stats")
        s_mv = sem("b_moments")
        s_sd = sem("b_deviation")
        s_rs = sem("b_reciprocal")
        s_yn = sem("b_normed")
        s_np = sem("b_normed_transposed")
        s_ns = sem("b_normed_scaled")
        s_mp = sem("b_mlp_hidden")
        s_ms = sem("b_mlp_silu")
        s_op = sem("b_mlp_out")
        s_o = sem("b_result")
        s_out = sem("b_stored")

        loads = [
            (w_gu[:], t["w_gu"]), (w_dn[:], t["w_dn"]), (ws_gu[:], t["ws_gu"]), (ws_dn[:], t["ws_dn"]),
            (m1[:], t["m1"]), (m2[:], t["m2"]), (m2b[:], t["m2b"]), (cols[:], t["cols"]), (ident[:], t["ident"]),
            (pick_hi[:], t["pick_hi"]), (pick_lo[:], t["pick_lo"]), (gather[:], t["gather"]),
            (own_hi[:], t["own_hi"]), (own_lo[:], t["own_lo"]),
        ]
        N_W = 16 * len(loads)

        def steps(engine, body):
            body(0, 0)
            body(1, 1)
            with engine.Fori(2, TILES - 1, 2) as k:
                body(k, 0)
                body(k + 1, 1)
            body(TILES - 1, 0)
            body(TILES, 1)
        assert TILES % 2 == 1

        with ExitStack() as setup:
            pos_w = cand[0][0:HALF, 0:2 * D]
            posT = cand[1][0:HALF + 1, 0:2 * E]
            pos_b = cand[2][0:1, 0:D]
            raw_w = kept[0][0:HALF, 0:2 * D]
            pe_l = kept[1][0:E, 0:D]
            pe_t = kept[2][0:HALF, 0:2 * E]
            with nc.Block() as block:
                @block.sync
                def _(sp):
                    for dst, src in loads:
                        sp.dma_start(dst, src).then_inc(s_w, 16)
                    sp.dma_start(pos_w, t["pos_w"]).then_inc(s_pe, 16)
                    sp.dma_start(posT[0:HALF, :], t["posT"]).then_inc(s_pe, 16)
                    sp.dma_start(pos_b, t["pos_b"]).then_inc(s_pe, 16)
                    sp.dma_start(raw_w, t["gate_w"]).then_inc(s_pe, 16)
                    for e in range(E):
                        sp.dma_start(gatew[HALF:HALF + 1, 1, e * D:(e + 1) * D], t["gate_b"]).then_inc(s_pe, 16)
                    sp.wait_ge(s_w, N_W)

                @block.gpsimd
                def _(pool):
                    nc.gpsimd.memset(xbd[:], 0.0)

                @block.vector
                def _(dve):
                    nc.vector.memset(eps[:], 1e-6)
                    nc.vector.memset(ones[:], 1.0)
                    nc.vector.memset(xt[HALF:HALF + 1, :, :], 1.0).then_inc(s_const, 1)
                    dve.wait_ge(s_pet, 1)
                    nc.vector.reduce_max(nmax[0:E, 0:1], p_misc[0:E, 0:D], mybir.AxisListType.X).then_inc(s_pet, 1)
                    dve.wait_ge(s_pet, 2)
                    nc.vector.tensor_scalar(nmax[0:E, 1:2], nmax[0:E, 0:1], -1.0, None, ALU.mult).then_inc(s_pet, 1)
                    dve.wait_ge(s_pet, 4)
                    nc.vector.reciprocal(rtotal[0:E, 0:1], total[0:E, 0:1]).then_inc(s_pet, 1)
                    dve.wait_ge(s_pet, 5)
                    nc.vector.tensor_scalar(pe_l, pe_l, rtotal[0:E, 0:1], None, ALU.mult).then_inc(s_pet, 1)
                    dve.wait_ge(s_pet, 7)
                    nc.vector.tensor_copy(pe_t, p_misc[0:HALF, 0:2 * E]).then_inc(s_pet, 1)
                    dve.wait_ge(s_pet, 8)
                    for e in range(E):
                        for f in range(2):
                            op = nc.vector.tensor_scalar(gatew[0:HALF, f, e * D:(e + 1) * D],
                                                         raw_w[:, f * D:(f + 1) * D],
                                                         pe_t[:, f * E + e:f * E + e + 1], None, ALU.mult)
                    op.then_inc(s_gw0, 1)

                @block.scalar
                def _(act):
                    act.wait_ge(s_pet, 3)
                    nc.scalar.activation(pe_l, p_misc[0:E, 0:D], ACT.Exp, bias=nmax[0:E, 1:2],
                                         accum_out=total[0:E, 0:1]).then_inc(s_pet, 1)

                @block.tensor
                def _(pe):
                    pe.wait_ge(s_w, N_W)
                    pe.wait_ge(s_pe, 16 * (4 + E))
                    pe.wait_ge(s_const, 1)
                    for f in range(2):
                        nc.tensor.matmul(p_misc[0:E, 0:D], posT[0:HALF, f * E:(f + 1) * E],
                                         pos_w[:, f * D:(f + 1) * D], start=f == 0, stop=False)
                    nc.tensor.matmul(p_misc[0:E, 0:D], ones[:, 0:E], pos_b, start=False, stop=True)\
                        .then_inc(s_pet, 1)
                    pe.wait_ge(s_pet, 6)
                    for f in range(2):
                        mm = nc.tensor.transpose(p_misc[0:HALF, f * E:(f + 1) * E],
                                                 pe_l[:, f * HALF:(f + 1) * HALF], ident[0:E, 0:E])
                    mm.then_inc(s_pet, 1)

        def is_first(k):
            return isinstance(k, int) and k == 0

        def is_last(k):
            return isinstance(k, int) and k == TILES

        with nc.Block() as block:
            @block.sync
            def _(sp):
                sp.dma_start(xin[:], x2_dram[0:128]).then_inc(s_xin, 16)

                def load_diagonal(tile, k):
                    wait(sp, s_cp, UNITS * (k - 1))
                    rows = x2_dram[bass.ds(128 * tile, 128)].rearrange(
                        "(g t) (h l) -> t h g l", t=GROUP, l=LO)
                    for b in range(GROUP):
                        sp.dma_start(xbd[b * HI:(b + 1) * HI, :, b, :], rows[b]).then_inc(s_bd, 16)

                def body(k, parity):
                    n = k - 1
                    if not is_last(k):
                        sp.wait_ge(s_xtp, k + 1)
                        sp.dma_start(xin[:], x2_dram[bass.ds(128 * (k + 1), 128)] if not is_first(k)
                                     else x2_dram[128:256]).then_inc(s_xin, 16)
                    if not is_first(k):
                        wait(sp, s_xsp, n)
                        sp.dma_start(xsh[:], x2_dram[bass.ds(128 * n, 128)]).then_inc(s_xsh, 16)
                        wait(sp, s_o, n)
                        sp.dma_start(h1t[:], h1_dram[bass.ds(128 * n, 128)]).then_inc(s_h1, 16)
                    if not is_last(k):
                        load_diagonal(k, k + 1)
                    if not is_first(k):
                        sp.wait_ge(s_o, k)
                        sp.dma_start(out[bass.ds(128 * n, 128)], res[:]).then_inc(s_out, 16)
                steps(sp, body)
                sp.wait_ge(s_out, 16 * TILES)

            @block.tensor
            def _(pe):
                def transposes(k):
                    pe.wait_ge(s_xin, 16 * (k + 2))
                    wait(pe, s_ns, k - 1)
                    wait(pe, s_g, GATES * (k + 1))
                    wait(pe, s_o, k - 1)
                    for f in range(2):
                        mm = nc.tensor.transpose(p_misc[0:HALF, f * 128:(f + 1) * 128],
                                                 xin[:, f * HALF:(f + 1) * HALF], ident[:])
                    mm.then_inc(s_xtp, 1)

                def gates(k, q):
                    if q == 0:
                        pe.wait_ge(s_xt, k + 2)
                    else:
                        pe.wait_ge(s_g, GATES * (k + 1) + q)
                    for f in range(2):
                        mm = nc.tensor.matmul(p_misc[:, 0:2 * D], xt[0:HALF + f, f, :],
                                              gatew[0:HALF + f, f, 2 * q * D:2 * (q + 1) * D],
                                              start=f == 0, stop=f == 1)
                    mm.then_inc(s_gp, 1)

                def broadcast(k, u):
                    done = UNITS * (k - 1)
                    at = slice((u % PARTS) * WIDE, (u % PARTS + 1) * WIDE)
                    if u == 0:
                        pe.wait_ge(s_cast, 2 * k)
                        wait(pe, s_a, BLOCKS * (k - 1))
                    wait(pe, s_hs, done + u)
                    nc.tensor.matmul(p_hi[0:GROUP * HI, :], pick_hi[:, u // PARTS, :], hi[:, at],
                                     start=True, stop=True).then_inc(s_hp, 1)
                    wait(pe, s_ls, done + u)
                    nc.tensor.matmul(p_lo[:, :], pick_lo[:, u // PARTS, :], lo[:, at],
                                     start=True, stop=True).then_inc(s_lp, 1)

                def candidates(k, u):
                    done = UNITS * (k - 1)
                    if u == 0:
                        pe.wait_ge(s_bd, 16 * GROUP * k)
                    if u < 2:
                        wait(pe, s_yn, k - 1)
                        wait(pe, s_ts, E // 4 * (k - 1))
                    wait(pe, s_cs, done + u - 1)
                    pe.wait_ge(s_hot, done + u + 1)
                    nc.tensor.matmul(p_cand[u % 2][:, :], xbd[:, u // PARTS].rearrange("p a b -> p (a b)"),
                                     hot[u % RING][:], start=True, stop=True).then_inc(s_cp, 1)

                def accumulate(k, u):
                    done = UNITS * (k - 1)
                    grp = u // PARTS
                    if u == 0:
                        wait(pe, s_gx, PARTS * (k - 1))
                    pe.wait_ge(s_kept, done + u + 1)
                    first = 128 - GROUP - GROUP * grp
                    nc.tensor.matmul(acc[u % PARTS][:, :], gather[:, first:first + 128], kept[u % RING][:],
                                     start=grp == 0, stop=grp == GROUPS - 1,
                                     skip_group_check=True).then_inc(s_acc, 1)

                def shared_transposes(k):
                    pe.wait_ge(s_xsh, 16 * k)
                    wait(pe, s_g, GATES * (k + 1) if is_last(k) else GATES * (k + 2))
                    for f in range(2):
                        mm = nc.tensor.transpose(p_misc[0:HALF, f * 128:(f + 1) * 128],
                                                 xsh[:, f * HALF:(f + 1) * HALF], ident[:])
                    mm.then_inc(s_xsp, 1)

                def expert_transposes(k, q):
                    if q == 0:
                        pe.wait_ge(s_gx, PARTS * k)
                    pe.wait_ge(s_cs, UNITS * k)
                    wait(pe, s_ts, E // 4 * (k - 1) + q)
                    for j in range(4):
                        mm = nc.tensor.transpose(p_t[0:K, j * 128:(j + 1) * 128], w[1 - parity_of[0]][:, 4 * q + j, :],
                                                 ident[:])
                    mm.then_inc(s_tp, 1)

                def hidden(k, b):
                    if b < 2:
                        pe.wait_ge(s_hs, UNITS * k)
                        pe.wait_ge(s_ls, UNITS * k)
                    wait(pe, s_a, BLOCKS * (k - 1) + b - 1)
                    dst = p_h[b % 2]
                    if b < SHARED:
                        pe.wait_ge(s_xss, k)
                        for m in range(4):
                            col = (m // 2) * SI + b * D + (m % 2) * HALF
                            for f in range(2):
                                mm = nc.tensor.matmul(dst[0:HALF, m * 128:(m + 1) * 128],
                                                      ws_gu[:, f, col:col + HALF], xst[:, f, :],
                                                      start=f == 0, stop=f == 1)
                    else:
                        e = b - SHARED
                        pe.wait_ge(s_ts, E // 4 * (k - 1) + e // 4 + 1)
                        for m in range(4):
                            mm = nc.tensor.matmul(dst[0:HALF, m * 128:(m + 1) * 128],
                                                  w_gu[:, e, m * HALF:(m + 1) * HALF], gwt[(e // 4) % 2][:, e % 4, :],
                                                  start=True, stop=True)
                    mm.then_inc(s_h, 1)

                def down(k, b):
                    if b == 0:
                        pe.wait_ge(s_cs, UNITS * k)
                    pe.wait_ge(s_a, BLOCKS * (k - 1) + b + 1)
                    for f in range(2):
                        wd = ws_dn[:, b, f, :] if b < SHARED else w_dn[:, b - SHARED, f, :]
                        mm = nc.tensor.matmul(p_y[:, 0:D], act_s[b % 2][:, f * 128:(f + 1) * 128], wd,
                                              start=b == 0 and f == 0, stop=b == BLOCKS - 1 and f == 1)
                    mm.then_inc(s_dn, 1)

                def tail(k):
                    pe.wait_ge(s_xss, k)
                    pe.wait_ge(s_yn, k)
                    for f in range(2):
                        mm = nc.tensor.transpose(p_misc[0:HALF, f * 128:(f + 1) * 128],
                                                 yn[:, f * HALF:(f + 1) * HALF], ident[:])
                    mm.then_inc(s_np, 1)
                    pe.wait_ge(s_ns, k)
                    for m in range(2):
                        for f in range(2):
                            mm = nc.tensor.matmul(p_misc[0:HALF, 256 + m * 128:256 + (m + 1) * 128],
                                                  m1[:, f, m * HALF:(m + 1) * HALF], ynt[:, f, :],
                                                  start=f == 0, stop=f == 1)
                    mm.then_inc(s_mp, 1)
                    pe.wait_ge(s_ms, k)
                    for f in range(2):
                        nc.tensor.matmul(p_misc[:, 0:D], mid[:, f, :], m2[:, f, :], start=f == 0, stop=False)
                    nc.tensor.matmul(p_misc[:, 0:D], ones[:, :], m2b[:, :], start=False, stop=True)\
                        .then_inc(s_op, 1)

                parity_of = [0]

                def body(k, parity):
                    parity_of[0] = parity
                    if not is_last(k):
                        transposes(k)
                    if is_first(k):
                        for q in range(GATES):
                            gates(k, q)
                        return
                    for u in range(-2, UNITS):
                        if u + 2 < UNITS:
                            broadcast(k, u + 2)
                        if 0 <= u + 1 < UNITS:
                            candidates(k, u + 1)
                        if u >= 0:
                            accumulate(k, u)
                        if u % 5 == 2 and u // 5 < GATES and not is_last(k):
                            gates(k, u // 5)
                    shared_transposes(k)
                    for b in range(BLOCKS + 1):
                        if b == SHARED:
                            expert_transposes(k, 0)
                        if b < BLOCKS:
                            hidden(k, b)
                        if b >= 1:
                            down(k, b - 1)
                        if b >= SHARED and (b - SHARED) % 4 == 0 and (b - SHARED) // 4 + 1 < E // 4:
                            expert_transposes(k, (b - SHARED) // 4 + 1)
                    tail(k)

                transposes(-1)
                for q in range(GATES):
                    gates(-1, q)
                steps(pe, body)

            @block.scalar
            def _(act):
                def copy_xt(k):
                    act.wait_ge(s_xtp, k + 2)
                    wait(act, s_gp, GATES * (k + 1))
                    nc.scalar.activation(xt[0:HALF].rearrange("p a b -> p (a b)"), p_misc[0:HALF, 0:256],
                                         ACT.Copy).then_inc(s_xt, 1)

                def copy_gates(k, q, parity):
                    act.wait_ge(s_gp, GATES * (k + 1) + q + 1)
                    nc.scalar.activation(g[1 - parity][:, 2 * q:2 * q + 2, :].rearrange("p a b -> p (a b)"),
                                         p_misc[:, 0:2 * D], ACT.Copy).then_inc(s_g, 1)

                def copy_hi(k, u):
                    act.wait_ge(s_hp, UNITS * (k - 1) + u + 1)
                    wait(act, s_hot, UNITS * (k - 1) + u + 1 - RING)
                    nc.scalar.activation(hi_s[u % RING][:], p_hi[0:GROUP * HI, :], ACT.Copy).then_inc(s_hs, 1)

                def copy_lo(k, u):
                    act.wait_ge(s_lp, UNITS * (k - 1) + u + 1)
                    wait(act, s_mask, UNITS * (k - 1) + u + 1 - RING)
                    nc.scalar.activation(lo_s[u % RING][:], p_lo[:, :], ACT.Copy).then_inc(s_ls, 1)

                def copy_candidates(k, u):
                    act.wait_ge(s_cp, UNITS * (k - 1) + u + 1)
                    wait(act, s_kept, UNITS * (k - 1) + u + 1 - RING)
                    nc.scalar.activation(cand[u % RING][:], p_cand[u % 2][:, :], ACT.Copy).then_inc(s_cs, 1)

                def body(k, parity):
                    p = 1 - parity
                    if not is_first(k):
                        act.wait_ge(s_idx, 2 * k)
                        nc.scalar.activation(hi[:], hi[:].bitcast(U16), ACT.Copy).then_inc(s_cast, 1)
                        nc.scalar.activation(lo[:], lo[:].bitcast(U16), ACT.Copy).then_inc(s_cast, 1)
                    if not is_last(k):
                        copy_xt(k)
                    if is_first(k):
                        for q in range(GATES):
                            copy_gates(k, q, parity)
                        return
                    for u in range(-2, UNITS):
                        if u + 2 < UNITS:
                            copy_hi(k, u + 2)
                            copy_lo(k, u + 2)
                        if 0 <= u + 1 < UNITS:
                            copy_candidates(k, u + 1)
                        if u == 3:
                            act.wait_ge(s_nmax, k)
                            for e in range(E):
                                op = nc.scalar.activation(w[p][:, e, :], w[p][:, e, :], ACT.Exp,
                                                          bias=nmax[:, e:e + 1], accum_out=total[:, e:e + 1])
                            op.then_inc(s_exp, 1)
                        if u % 5 == 2 and u // 5 < GATES and not is_last(k):
                            copy_gates(k, u // 5, parity)
                    act.wait_ge(s_xsp, k)
                    nc.scalar.activation(xst[:].rearrange("p a b -> p (a b)"), p_misc[0:HALF, 0:256],
                                         ACT.Copy).then_inc(s_xss, 1)
                    def copy_t(q):
                        act.wait_ge(s_tp, E // 4 * (k - 1) + q + 1)
                        if q >= 2:
                            act.wait_ge(s_h, BLOCKS * (k - 1) + SHARED + 4 * (q - 1))
                        nc.scalar.activation(gwt[q % 2][:].rearrange("p a b -> p (a b)"), p_t[0:K, :],
                                             ACT.Copy).then_inc(s_ts, 1)
                    for b in range(BLOCKS):
                        if b == SHARED:
                            copy_t(0)
                        act.wait_ge(s_h, BLOCKS * (k - 1) + b + 1)
                        wait(act, s_a, BLOCKS * (k - 1) + b - 1)
                        nc.scalar.activation(silu[b % 2][:], p_h[b % 2][0:HALF, 0:256], ACT.Silu).then_inc(s_si, 1)
                        if b >= SHARED and (b - SHARED) % 4 == 0 and (b - SHARED) // 4 + 1 < E // 4:
                            copy_t((b - SHARED) // 4 + 1)
                    act.wait_ge(s_mv, k)
                    nc.scalar.activation(sd[:], mv[:, 1:2], ACT.Sqrt, bias=eps[:]).then_inc(s_sd, 1)
                    act.wait_ge(s_np, k)
                    for f in range(2):
                        op = nc.scalar.activation(ynt[:, f, :], p_misc[0:HALF, f * 128:(f + 1) * 128], ACT.Identity,
                                                  scale=cols[:, f:f + 1], bias=cols[:, 2 + f:3 + f])
                    op.then_inc(s_ns, 1)
                    act.wait_ge(s_mp, k)
                    for f in range(2):
                        op = nc.scalar.activation(mid[:, f, :], p_misc[0:HALF, 256 + f * 128:256 + (f + 1) * 128],
                                                  ACT.Silu, bias=cols[:, 4 + f:5 + f])
                    op.then_inc(s_ms, 1)

                copy_xt(-1)
                for q in range(GATES):
                    copy_gates(-1, q, 1)
                steps(act, body)

            @block.gpsimd
            def _(pool):
                def body(k, parity):
                    if is_first(k):
                        return
                    done = UNITS * (k - 1)

                    def mark(u):
                        pool.wait_ge(s_hs, done + u + 1)
                        wait(pool, s_cp, done + u + 1 - RING)
                        pool.sem_inc(s_held, 1)
                        nc.gpsimd.tensor_scalar(hot[u % RING][:], hi_s[u % RING][:], own_hi[:, 0:1], None,
                                                ALU.is_equal).then_inc(s_hot, 1)
                        pool.wait_ge(s_ls, done + u + 1)
                        wait(pool, s_acc, done + u + 1 - RING)
                        pool.sem_inc(s_held, 1)
                        nc.gpsimd.tensor_scalar(kept[u % RING][:], lo_s[u % RING][:], own_lo[:, 0:1], None,
                                                ALU.is_equal).then_inc(s_mask, 1)

                    def keep(u):
                        pool.wait_ge(s_mask, done + u + 1)
                        pool.wait_ge(s_cs, done + u + 1)
                        nc.gpsimd.tensor_tensor(kept[u % RING][:], kept[u % RING][:], cand[u % RING][:],
                                                ALU.mult).then_inc(s_kept, 1)
                    for u in range(UNITS + 1):
                        if u < UNITS:
                            mark(u)
                        if u >= 1:
                            keep(u - 1)
                steps(pool, body)

            @block.vector
            def _(dve):
                def start(k, parity):
                    p = 1 - parity
                    dve.wait_ge(s_sort, SORT_INCS)
                    dve.sem_clear(s_sort)
                    wait(dve, s_lp, UNITS * (k - 1))
                    flat = idx[:].rearrange("p a b -> p (a b)")
                    nc.vector.tensor_scalar(hi[:].bitcast(U16), flat, 4, None,
                                            ALU.logical_shift_right).then_inc(s_idx, 1)
                    nc.vector.tensor_scalar(lo[:].bitcast(U16), flat, LO - 1, None,
                                            ALU.bitwise_and).then_inc(s_idx, 1)
                    nc.vector.tensor_scalar(nmax[:], w[p][:, :, 0], -1.0, None, ALU.mult).then_inc(s_nmax, 1)

                def normalise(k, p):
                    dve.wait_ge(s_exp, k)
                    nc.vector.reciprocal(rtotal[:], total[:]).then_inc(s_rt, 1)
                    dve.wait_ge(s_rt, k)
                    nc.vector.tensor_tensor(w[p][:], w[p][:], rtotal[:].unsqueeze(2).to_broadcast([128, E, K]),
                                            ALU.mult).then_inc(s_wt, 1)

                def weigh(k, p, c):
                    if c == 0:
                        dve.wait_ge(s_wt, k)
                        dve.wait_ge(s_acc, UNITS * k)
                    flat = w[p][:].rearrange("p a b -> p (a b)")[:, c * WIDE:(c + 1) * WIDE]
                    nc.vector.tensor_tensor(flat, acc[c][:, :], flat, ALU.mult).then_inc(s_gx, 1)

                def activate(k, b):
                    dve.wait_ge(s_si, BLOCKS * (k - 1) + b + 1)
                    wait(dve, s_dn, BLOCKS * (k - 1) + b - 1)
                    nc.vector.tensor_tensor(act_s[b % 2][:], silu[b % 2][:], p_h[b % 2][0:HALF, 256:512],
                                            ALU.mult).then_inc(s_a, 1)

                def norm_stats(k):
                    dve.wait_ge(s_dn, BLOCKS * k)
                    nc.vector.bn_stats(stats[:], p_y[:, 0:D]).then_inc(s_st, 1)

                def norm_moments(k):
                    dve.wait_ge(s_st, k)
                    dve.sem_inc(s_held_v, 1)
                    nc.vector.bn_aggr(mv[:], stats[:]).then_inc(s_mv, 1)

                def norm_reciprocal(k):
                    dve.wait_ge(s_sd, k)
                    nc.vector.reciprocal(rstd[:], sd[:]).then_inc(s_rs, 1)

                def norm_apply(k):
                    dve.wait_ge(s_rs, k)
                    nc.vector.tensor_scalar(yn[:], p_y[:, 0:D], mv[:, 0:1], rstd[:, 0:1], ALU.subtract,
                                            ALU.mult).then_inc(s_yn, 1)

                def residual(k):
                    dve.wait_ge(s_h1, 16 * k)
                    wait(dve, s_out, 16 * (k - 1))
                    dve.wait_ge(s_op, k)
                    nc.vector.tensor_tensor(res[:], p_misc[:, 0:D], h1t[:], ALU.add).then_inc(s_o, 1)

                def body(k, parity):
                    p = 1 - parity
                    if not is_first(k):
                        start(k, parity)
                    if not is_last(k):
                        wait(dve, s_tp, E // 4 * (k - 1))
                        dve.wait_ge(s_g, GATES * (k + 1))
                        nc.vector.tensor_copy(carrier[:], eps[:])
                    incs = 0
                    for step in range(ROUNDS * E // 2):
                        pair, r = step // ROUNDS, step % ROUNDS
                        if not is_last(k):
                            feats = [g[parity][:, 2 * pair + i, :] for i in range(2)]
                            tops = [w[parity][:, 2 * pair + i, 8 * r:8 * r + 8] for i in range(2)]
                            for i in range(2):
                                if r:
                                    dve.wait_ge(s_sort, incs - 1)
                                nc.vector.max(tops[i], feats[i]).then_inc(s_sort, 1)
                                incs += 1
                            for i in range(2):
                                dve.wait_ge(s_sort, incs - 1 + i)
                                nc.vector.max_index(idx[:, 2 * pair + i, 8 * r:8 * r + 8], tops[i], feats[i])
                            for i in range(2):
                                nc.vector.match_replace(feats[i], tops[i], feats[i], LOWEST).then_inc(s_sort, 1)
                                incs += 1
                        if is_first(k):
                            continue
                        if step == 8:
                            normalise(k, p)
                        if step == 71:
                            for c in range(PARTS):
                                weigh(k, p, c)
                        if 72 <= step < 72 + BLOCKS:
                            activate(k, step - 72)
                        if step == 91:
                            norm_stats(k)
                            norm_moments(k)
                        if step == 92:
                            norm_reciprocal(k)
                            norm_apply(k)
                        if step == 95:
                            residual(k)
                steps(dve, body)


def build(nc, t, out):
    h1_dram = nc.dram_tensor("h1_scratch", [PADDED, D], F32, kind="Internal").ap()
    x2_dram = nc.dram_tensor("x2_scratch", [PADDED, D], F32, kind="Internal").ap()
    phase_a(nc, t, h1_dram, x2_dram)
    phase_b(nc, t, h1_dram, x2_dram, out)


def kernel(**inputs):
    import ml_dtypes
    import numpy as np
    import concourse.bacc as bacc
    from concourse.bass_utils import run_bass_kernel_spmd

    a = {n.replace("L0_", "").replace("ffn_", "").replace("attn_", ""): np.asarray(v) for n, v in inputs.items()}

    def chunked(m, p=HALF):
        return m.reshape(-1, p, m.shape[-1]).transpose(1, 0, 2)

    x = a["x"].reshape(IMAGES, CHANNELS, SIDE, PATCH, SIDE, PATCH).transpose(0, 1, 3, 5, 2, 4)
    x = x.reshape(IMAGES, PC, 128, SIDE * SIDE).transpose(0, 2, 1, 3)
    patches = np.zeros((IMAGES, 128, PC, TOKENS), x.dtype)
    patches[..., 1:] = x
    base = np.zeros((2 * CHUNK[0], D), x.dtype)
    base[:] = a["tok_b_lin"]
    base[0] = a["tok_cls_token"][0]
    wkv = np.zeros((2, HALF + 1, 2 * D), x.dtype)
    wkv[:, :HALF] = np.concatenate([a["Wk"].T, a["Wv"].T], axis=1).reshape(2, HALF, 2 * D)
    wkv[1, HALF] = np.concatenate([a["bk"], a["bv"]])
    tok = np.arange(128)
    pick = {n: (tok[:, None] == np.repeat(tok, n)[None, :]).reshape(128, GROUPS, GROUP * n)
            for n in (HI, LO)}
    gather = (np.arange(2 * 128 - GROUP)[None, :] - (128 - GROUP)) == (np.arange(GROUP * LO) // LO)[:, None]
    t = {
        "patches": patches,
        "w_lin": a["tok_W_lin"].T,
        "base": base.reshape(2, CHUNK[0], D),
        "wq": a["Wq"].T,
        "bq": a["bq"].reshape(2, HALF).T,
        "wkv": wkv,
        "ident": np.eye(128, dtype=np.float32),
        "pos_w": chunked(a["pos_w"]).reshape(HALF, 2 * D),
        "posT": chunked(a["posembed"].T).reshape(HALF, 2 * E),
        "pos_b": a["pos_b"][None],
        "gate_w": chunked(a["gate_w"]).reshape(HALF, 2 * D),
        "gate_b": a["gate_b"][None],
        "w_gu": np.concatenate([a["eg_w"], a["eu_w"]], axis=2).transpose(1, 0, 2),
        "w_dn": a["ed_w"].reshape(E, 2, HALF, D).transpose(2, 0, 1, 3),
        "ws_gu": chunked(np.concatenate([a["sg_w"], a["su_w"]], axis=1)),
        "ws_dn": a["sd_w"].reshape(SHARED, 2, HALF, D).transpose(2, 0, 1, 3),
        "m1": chunked(a["m1_w"]),
        "m2": chunked(a["m2_w"]),
        "m2b": a["m2_b"][None],
        "cols": np.concatenate([a[n].reshape(2, HALF) for n in ("ln_g", "ln_b", "m1_b")]).T,
        "pick_hi": pick[HI].astype(ml_dtypes.bfloat16),
        "pick_lo": pick[LO].astype(ml_dtypes.bfloat16),
        "gather": gather.astype(np.float32),
        "own_hi": (np.arange(GROUP * HI) % HI).astype(np.float32)[:, None],
        "own_lo": (np.arange(GROUP * LO) % LO).astype(np.float32)[:, None],
    }
    nc = bacc.Bacc("TRN2", target_bir_lowering=False, num_devices=1)
    arrays, aps = {}, {}
    for name, value in t.items():
        value = np.ascontiguousarray(value)
        arrays[f"in_{name}"] = value
        aps[name] = nc.dram_tensor(f"in_{name}", value.shape, mybir.dt.from_np(value.dtype),
                                   kind="ExternalInput").ap()
    out = nc.dram_tensor("out_rows", [TILES * 128, D], F32, kind="ExternalOutput").ap()
    build(nc, aps, out)
    result = run_bass_kernel_spmd(nc, [arrays], core_ids=[0]).results[0]["out_rows"]
    return result[:ROWS].reshape(IMAGES, TOKENS, D)
```

```python
from contextlib import ExitStack

import concourse.bass as bass
from concourse import mybir

ALU = mybir.AluOpType
ACT = mybir.ActivationFunctionType
F32 = mybir.dt.float32
BF16 = mybir.dt.bfloat16
U16 = mybir.dt.uint16

IMAGES, SIDE, PATCH, CHANNELS = 64, 14, 16, 3
TOKENS = SIDE * SIDE + 1
PATCH_DIM = CHANNELS * PATCH * PATCH
PC = PATCH_DIM // 128
D = 192
HALF = D // 2
CHUNK = [99, 98]
E = 16
K = D // 2
SI = 2 * D
ROUNDS = K // 8
ROWS = IMAGES * TOKENS
TILES = -(-ROWS // 128)
PADDED = (TILES + 1) * 128
LO, HI = 16, D // 16
GROUP = 8
GROUPS = 128 // GROUP
WIDE = 512
PARTS = E * K // WIDE
UNITS = GROUPS * PARTS
RING = 4
LAG = 3
SHARED = SI // D
BLOCKS = E + SHARED
WEIGH = 69
GATES = E // 2
LOWEST = -3.0e38
SORT_INCS = 2 * 2 * ROUNDS * (E // 2)
PER_STEP = 4
STEPS_A = IMAGES // PER_STEP
SPLIT = 3


def wait(engine, semaphore, value):
    if isinstance(value, int) and value <= 0:
        return
    engine.wait_ge(semaphore, value)


def masks(k, u):
    return UNITS // 2 * (k - 1) + (u + 1) // 2


def phase_a(nc, t, h1_dram, x2_dram, parts_dram):
    with ExitStack() as ctx:
        def sb(name, shape, dt=F32):
            return ctx.enter_context(nc.sbuf_tensor(name, shape, dt))

        def sem(name):
            return ctx.enter_context(nc.semaphore(name))

        n_img = PER_STEP
        wlin = sb("wlin", [128, PC, D])
        base = sb("base", [CHUNK[0], 2, D])
        wq = sb("wq", [HALF, 2, D])
        bq = sb("bq", [HALF, 2])
        wkv = sb("wkv", [HALF + 1, 2, 2 * D])
        ident = sb("ident_a", [128, 128])
        eps = sb("eps_a", [128, 1])
        zeros = sb("zeros", [128, D])
        patches = [sb(f"patches{i}", [128, PC, TOKENS]) for i in range(n_img)]
        h0 = [sb(f"h0_{i}", [CHUNK[0], 2, D]) for i in range(n_img)]
        stats = [sb(f"stats{i}", [CHUNK[0], 2, 6]) for i in range(n_img)]
        mv = [sb(f"mv{i}", [CHUNK[0], 2, 2]) for i in range(n_img)]
        sd = [sb(f"sd{i}", [CHUNK[0], 2]) for i in range(n_img)]
        rstd = [sb(f"rstd{i}", [CHUNK[0], 2]) for i in range(n_img)]
        xn = [sb(f"xn{i}", [CHUNK[0], 2, D]) for i in range(n_img)]
        xnt = [sb(f"xnt{i}", [HALF + 1, 2, TOKENS]) for i in range(n_img)]
        qt = [sb(f"qt{i}", [HALF, 2, TOKENS]) for i in range(n_img)]
        kv = [sb(f"kv{i}", [CHUNK[0], 2, 2 * D]) for i in range(n_img)]
        kvm = [sb(f"kvm{i}", [HALF, 2, D]) for i in range(n_img)]
        h1 = [sb(f"h1_{i}", [CHUNK[0], 2, D]) for i in range(n_img)]
        x2 = [sb(f"x2_{i}", [CHUNK[0], 2, D]) for i in range(n_img)]
        parts = [sb(f"parts{i}", [CHUNK[0], SPLIT, 2, D], BF16) for i in range(n_img)]
        rest = [sb(f"rest{i}", [CHUNK[0], 2, D]) for i in range(n_img)]
        pa = [ctx.enter_context(nc.psum_tensor(f"pa{i}", [128, WIDE], F32)) for i in range(n_img)]
        pb = [ctx.enter_context(nc.psum_tensor(f"pb{i}", [128, WIDE], F32)) for i in range(n_img)]

        s_w = sem("a_weights")
        s_zero = sem("a_zeros")
        s_eps = sem("a_eps")
        s_held = sem("a_vector_waits_passed")
        s_ones = sem("a_ones_row")
        s_in = [sem(f"a_patches_loaded{i}") for i in range(n_img)]
        s_emb = sem("a_embedded")
        s_h0 = sem("a_h0")
        s_st = sem("a_stats")
        s_mv = sem("a_moments")
        s_sd = sem("a_deviation")
        s_rs = sem("a_reciprocal")
        s_xn = sem("a_normed")
        s_xtp = sem("a_transposed")
        s_xt = sem("a_transpose_copied")
        s_q = sem("a_q_product")
        s_qt = sem("a_q_copied")
        s_kvp = sem("a_kv_product")
        s_kv = sem("a_kv_copied")
        s_mp = sem("a_memory_product")
        s_m = sem("a_memory_copied")
        s_op = sem("a_attended")
        s_h1 = sem("a_h1")
        s_st2 = sem("a_stats2")
        s_mv2 = sem("a_moments2")
        s_sd2 = sem("a_deviation2")
        s_rs2 = sem("a_reciprocal2")
        s_x2 = sem("a_normed2")
        s_part = sem("a_parts")
        s_pad = sem("a_padding_stored")
        s_out = sem("a_stored")
        N_W = 6 * 16

        def steps(engine, body):
            body(0)
            with engine.Fori(1, STEPS_A - 1) as it:
                body(it)
            body(STEPS_A - 1)

        with nc.Block() as block:
            @block.sync
            def _(sp):
                sp.dma_start(wlin[:], t["w_lin"].rearrange("(c p) n -> p c n", p=128)).then_inc(s_w, 16)
                sp.dma_start(base[:], t["base"].rearrange("c p n -> p c n")).then_inc(s_w, 16)
                sp.dma_start(wq[:], t["wq"].rearrange("(c p) n -> p c n", p=HALF)).then_inc(s_w, 16)
                sp.dma_start(bq[:], t["bq"]).then_inc(s_w, 16)
                sp.dma_start(wkv[:], t["wkv"].rearrange("c p n -> p c n")).then_inc(s_w, 16)
                sp.dma_start(ident[:], t["ident"]).then_inc(s_w, 16)

                def load(it):
                    for i in range(n_img):
                        wait(sp, s_emb, n_img * (it - 1) + i + 1)
                        sp.dma_start(patches[i][:], t["patches"][bass.ds(n_img * it + i, 1)]
                                     .rearrange("a p c n -> (a p) c n")).then_inc(s_in[i], 16)

                sp.wait_ge(s_zero, 1)
                for first in range(ROWS, PADDED, 64):
                    sp.dma_start(h1_dram[first:first + 64], zeros[0:64, :]).then_inc(s_pad, 16)
                    sp.dma_start(x2_dram[first:first + 64], zeros[0:64, :]).then_inc(s_pad, 16)
                    for m in range(SPLIT):
                        sp.dma_start(parts_dram[m, first:first + 64], zeros[0:64, 0:HALF].bitcast(BF16))\
                            .then_inc(s_pad, 16)
                sp.wait_ge(s_pad, 16 * (2 + SPLIT) * (PADDED - ROWS) // 64)
                load(0)

                def body(it):
                    if not isinstance(it, int) or it < STEPS_A - 1:
                        load(it + 1)
                    for i in range(n_img):
                        row = TOKENS * (n_img * it + i)
                        sp.wait_ge(s_part, 4 * (n_img * it + i + 1))
                        for c, size in enumerate(CHUNK):
                            rows = bass.ds(row + c * CHUNK[0], size)
                            sp.dma_start(h1_dram[rows], h1[i][0:size, c, :]).then_inc(s_out, 16)
                            sp.dma_start(x2_dram[rows], x2[i][0:size, c, :]).then_inc(s_out, 16)
                            sp.dma_start(parts_dram[:, rows].rearrange("m p n -> p m n"),
                                         parts[i][0:size, :, c, :]).then_inc(s_out, 16)
                steps(sp, body)
                sp.wait_ge(s_out, 16 * 6 * IMAGES)

            @block.gpsimd
            def _(pool):
                nc.gpsimd.memset(zeros[:], 0.0).then_inc(s_zero, 1)

                def body(it):
                    for i in range(n_img):
                        pool.wait_ge(s_x2, n_img * it + i + 1)
                        seen = 4 * (n_img * it + i)
                        for c, size in enumerate(CHUNK):
                            op = nc.gpsimd.tensor_tensor(parts[i][0:size, 0, c, :], x2[i][0:size, c, :],
                                                         zeros[0:size, :], ALU.add)
                        op.then_inc(s_part, 1)
                        pool.wait_ge(s_part, seen + 1)
                        for c, size in enumerate(CHUNK):
                            op = nc.gpsimd.tensor_tensor(rest[i][0:size, c, :], x2[i][0:size, c, :],
                                                         parts[i][0:size, 0, c, :], ALU.subtract)
                        op.then_inc(s_part, 1)
                        pool.wait_ge(s_part, seen + 2)
                        for c, size in enumerate(CHUNK):
                            op = nc.gpsimd.tensor_tensor(parts[i][0:size, 1, c, :], rest[i][0:size, c, :],
                                                         zeros[0:size, :], ALU.add)
                        op.then_inc(s_part, 1)
                        pool.wait_ge(s_part, seen + 3)
                        for c, size in enumerate(CHUNK):
                            op = nc.gpsimd.tensor_tensor(parts[i][0:size, 2, c, :], rest[i][0:size, c, :],
                                                         parts[i][0:size, 1, c, :], ALU.subtract)
                        op.then_inc(s_part, 1)
                steps(pool, body)

            @block.tensor
            def _(pe):
                pe.wait_ge(s_w, N_W)

                def body(it):
                    def n(i):
                        return n_img * it + i + 1
                    for i in range(n_img):
                        wait(pe, s_qt, n(i) - n_img)
                        wait(pe, s_kv, 2 * (n(i) - n_img))
                        pe.wait_ge(s_in[i], 16 * (it + 1))
                        for c, size in enumerate(CHUNK):
                            for p in range(PC):
                                mm = nc.tensor.matmul(pa[i][0:size, c * D:(c + 1) * D],
                                                      patches[i][:, p, c * CHUNK[0]:c * CHUNK[0] + size],
                                                      wlin[:, p, :], start=p == 0, stop=p == PC - 1)
                        mm.then_inc(s_emb, 1)
                    for i in range(n_img):
                        wait(pe, s_h1, n(i) - n_img)
                        pe.wait_ge(s_xn, n(i))
                        for f in range(2):
                            for c, size in enumerate(CHUNK):
                                at = f * TOKENS + c * CHUNK[0]
                                mm = nc.tensor.transpose(pb[i][0:HALF, at:at + size],
                                                         xn[i][0:size, c, f * HALF:(f + 1) * HALF],
                                                         ident[0:size, 0:size])
                        mm.then_inc(s_xtp, 1)
                    for i in range(n_img):
                        pe.wait_ge(s_h0, n(i))
                        pe.wait_ge(s_ones, 1)
                        pe.wait_ge(s_xt, n(i))
                        for e in range(2):
                            for f in range(2):
                                mm = nc.tensor.matmul(pa[i][0:HALF, e * TOKENS:(e + 1) * TOKENS],
                                                      wq[:, f, e * HALF:(e + 1) * HALF], xnt[i][0:HALF, f, :],
                                                      start=f == 0, stop=f == 1)
                        mm.then_inc(s_q, 1)
                    for i in range(n_img):
                        for c, size in enumerate(CHUNK):
                            if c:
                                pe.wait_ge(s_qt, n(i))
                            out = (pb, pa)[c][i]
                            for f in range(2):
                                mm = nc.tensor.matmul(out[0:size, 0:2 * D],
                                                      xnt[i][0:HALF + f, f, c * CHUNK[0]:c * CHUNK[0] + size],
                                                      wkv[0:HALF + f, f, :], start=f == 0, stop=f == 1)
                            mm.then_inc(s_kvp, 1)
                    for i in range(n_img):
                        pe.wait_ge(s_kv, 2 * n(i))
                        for f in range(2):
                            for c, size in enumerate(CHUNK):
                                mm = nc.tensor.matmul(pb[i][0:HALF, f * D:(f + 1) * D],
                                                      kv[i][0:size, c, f * HALF:(f + 1) * HALF],
                                                      kv[i][0:size, c, D:2 * D], start=c == 0, stop=c == 1)
                        mm.then_inc(s_mp, 1)
                    for i in range(n_img):
                        pe.wait_ge(s_m, n(i))
                        for c, size in enumerate(CHUNK):
                            for f in range(2):
                                mm = nc.tensor.matmul(pb[i][0:size, c * D:(c + 1) * D],
                                                      qt[i][:, f, c * CHUNK[0]:c * CHUNK[0] + size],
                                                      kvm[i][:, f, :], start=f == 0, stop=f == 1)
                        mm.then_inc(s_op, 1)
                steps(pe, body)

            @block.vector
            def _(dve):
                nc.vector.memset(eps[:], 1e-5).then_inc(s_eps, 1)
                for i in range(n_img):
                    op = nc.vector.memset(xnt[i][HALF:HALF + 1, :, :], 1.0)
                op.then_inc(s_ones, 1)
                dve.wait_ge(s_w, N_W)

                def norm(it, src, dst, s_src, s_stat, s_mom, s_dev, s_rec, s_dst):
                    def n(i):
                        return n_img * it + i + 1
                    for i in range(n_img):
                        dve.wait_ge(s_src, n(i))
                        wait(dve, s_dst, n(i) - n_img)
                        for c, size in enumerate(CHUNK):
                            op = nc.vector.bn_stats(stats[i][0:size, c, :], src[i][0:size, c, :])
                        op.then_inc(s_stat, 1)
                    for i in range(n_img):
                        dve.wait_ge(s_stat, n(i))
                        dve.sem_inc(s_held, 1)
                        for c, size in enumerate(CHUNK):
                            op = nc.vector.bn_aggr(mv[i][0:size, c, :], stats[i][0:size, c, :])
                        op.then_inc(s_mom, 1)
                    for i in range(n_img):
                        dve.wait_ge(s_dev, n(i))
                        for c, size in enumerate(CHUNK):
                            op = nc.vector.reciprocal(rstd[i][0:size, c:c + 1], sd[i][0:size, c:c + 1])
                        op.then_inc(s_rec, 1)
                    for i in range(n_img):
                        dve.wait_ge(s_rec, n(i))
                        for c, size in enumerate(CHUNK):
                            op = nc.vector.tensor_scalar(dst[i][0:size, c, :], src[i][0:size, c, :],
                                                         mv[i][0:size, c, 0:1], rstd[i][0:size, c:c + 1],
                                                         ALU.subtract, ALU.mult)
                        op.then_inc(s_dst, 1)

                def body(it):
                    def n(i):
                        return n_img * it + i + 1
                    for i in range(n_img):
                        dve.wait_ge(s_emb, n(i))
                        for c, size in enumerate(CHUNK):
                            op = nc.vector.tensor_tensor(h0[i][0:size, c, :], pa[i][0:size, c * D:(c + 1) * D],
                                                         base[0:size, c, :], ALU.add)
                        op.then_inc(s_h0, 1)
                    norm(it, h0, xn, s_h0, s_st, s_mv, s_sd, s_rs, s_xn)
                    for i in range(n_img):
                        for c, size in enumerate(CHUNK):
                            dve.wait_ge(s_kvp, 2 * (n(i) - 1) + c + 1)
                            nc.vector.tensor_copy(kv[i][0:size, c, :], (pb, pa)[c][i][0:size, 0:2 * D])\
                                .then_inc(s_kv, 1)
                    for i in range(n_img):
                        if i == 0 and not (isinstance(it, int) and it == 0):
                            dve.wait_ge(s_out, 16 * 6 * n_img * it)
                        dve.wait_ge(s_op, n(i))
                        for c, size in enumerate(CHUNK):
                            op = nc.vector.tensor_tensor(h1[i][0:size, c, :], pb[i][0:size, c * D:(c + 1) * D],
                                                         h0[i][0:size, c, :], ALU.add)
                        op.then_inc(s_h1, 1)
                    norm(it, h1, x2, s_h1, s_st2, s_mv2, s_sd2, s_rs2, s_x2)
                steps(dve, body)

            @block.scalar
            def _(act):
                act.wait_ge(s_eps, 1)
                act.wait_ge(s_w, N_W)

                def body(it):
                    def n(i):
                        return n_img * it + i + 1
                    for i in range(n_img):
                        act.wait_ge(s_mv, n(i))
                        for c, size in enumerate(CHUNK):
                            op = nc.scalar.activation(sd[i][0:size, c:c + 1], mv[i][0:size, c, 1:2], ACT.Sqrt,
                                                      bias=eps[0:size, :])
                        op.then_inc(s_sd, 1)
                    for i in range(n_img):
                        act.wait_ge(s_xtp, n(i))
                        nc.scalar.activation(xnt[i][0:HALF, :, :].rearrange("p a b -> p (a b)"),
                                             pb[i][0:HALF, 0:2 * TOKENS], ACT.Copy).then_inc(s_xt, 1)
                    for i in range(n_img):
                        act.wait_ge(s_q, n(i))
                        for e in range(2):
                            op = nc.scalar.activation(qt[i][:, e, :], pa[i][0:HALF, e * TOKENS:(e + 1) * TOKENS],
                                                      ACT.Identity, bias=bq[:, e:e + 1])
                        op.then_inc(s_qt, 1)
                    for i in range(n_img):
                        act.wait_ge(s_mp, n(i))
                        nc.scalar.activation(kvm[i][:].rearrange("p a b -> p (a b)"), pb[i][0:HALF, 0:2 * D],
                                             ACT.Copy, scale=float(D) ** -0.5).then_inc(s_m, 1)
                    for i in range(n_img):
                        act.wait_ge(s_mv2, n(i))
                        for c, size in enumerate(CHUNK):
                            op = nc.scalar.activation(sd[i][0:size, c:c + 1], mv[i][0:size, c, 1:2], ACT.Sqrt,
                                                      bias=eps[0:size, :])
                        op.then_inc(s_sd2, 1)
                steps(act, body)


def phase_b(nc, t, h1_dram, x2_dram, parts_dram, out):
    with ExitStack() as ctx:
        def sb(name, shape, dt=F32):
            return ctx.enter_context(nc.sbuf_tensor(name, shape, dt))

        def sem(name):
            return ctx.enter_context(nc.semaphore(name))

        gatew = sb("gatew", [HALF + 1, 2, E * D])
        w_gu = sb("w_gu", [K, E, 2 * D])
        w_dn = sb("w_dn", [HALF, E, 2, D])
        ws_gu = sb("ws_gu", [HALF, 2, 2 * SI])
        ws_dn = sb("ws_dn", [HALF, SHARED, 2, D])
        m1 = sb("m1", [HALF, 2, D])
        m2 = sb("m2", [HALF, 2, D])
        m2b = sb("m2b", [1, D])
        cols = sb("cols", [HALF, 6])
        ident = sb("ident_b", [128, 128])
        pick = sb("pick", [128, GROUPS, 128], BF16)
        gather = sb("gather", [128, 2 * 128 - GROUP])
        minus_slot = sb("minus_slot", [128, 1])
        ones = sb("ones", [1, 128])
        eps = sb("eps_b", [128, 1])
        xin = sb("xin", [128, D])
        xsh = sb("xsh", [128, D])
        h1t = sb("h1t", [128, D])
        xt = sb("xt", [HALF + 1, 2, 128])
        xst = sb("xst", [HALF, 2, 128])
        g = [sb(f"g{b}", [128, E, D]) for b in range(2)]
        w = [sb(f"w{b}", [128, E, K]) for b in range(2)]
        idx = sb("idx", [128, E, K], U16)
        hi = sb("hi", [128, E * K], BF16)
        lo = sb("lo", [128, E * K], BF16)
        nmax = sb("nmax", [128, E])
        total = sb("total", [128, E])
        rtotal = sb("rtotal", [128, E])
        xbd = sb("xbd", [128, SPLIT, GROUPS, GROUP, LO], BF16)
        dist = [sb(f"dist{r}", [128, 2, WIDE], BF16) for r in range(RING)]
        marks = [sb(f"marks{r}", [128, 2, WIDE], BF16) for r in range(RING)]
        cand = [sb(f"cand{r}", [128, WIDE]) for r in range(RING)]
        kept = [sb(f"kept{r}", [128, WIDE]) for r in range(RING)]
        gwt = [sb(f"gwt{b}", [K, 4, 128]) for b in range(2)]
        silu = [sb(f"silu{b}", [HALF, 2 * 128]) for b in range(2)]
        act_s = [sb(f"act{b}", [HALF, 2 * 128]) for b in range(2)]
        carrier = sb("carrier", [128, 1])
        stats = sb("stats_b", [128, 6])
        mv = sb("mv_b", [128, 2])
        sd = sb("sd_b", [128, 1])
        rstd = sb("rstd_b", [128, 1])
        yn = sb("yn", [128, D])
        ynt = sb("ynt", [HALF, 2, 128])
        mid = sb("mid", [HALF, 2, 128])
        res = sb("res", [128, D])

        def bank(name, n=1):
            return ctx.enter_context(nc.psum_tensor(name, [128, n, WIDE], F32))
        acc = bank("acc", PARTS)
        pair = bank("pair", 2)
        p_cand = bank("p_cand", 2)
        p_misc = bank("p_misc")[:, 0]
        p_t, p_y = p_cand[:, 0], p_cand[:, 1]

        s_w = sem("b_weights")
        s_const = sem("b_constants")
        s_held = sem("b_pool_waits_passed")
        s_held_v = sem("b_vector_waits_passed")
        s_held_sp = sem("b_load_waits_passed")
        s_pe = sem("b_posembed")
        s_pet = sem("b_posembed_steps")
        s_gw0 = sem("b_gate_weights")
        s_xin = sem("b_x_loaded")
        s_xsh = sem("b_shared_x_loaded")
        s_h1 = sem("b_h1_loaded")
        s_bd = sem("b_block_diagonal_loaded")
        s_xtp = sem("b_x_transposed")
        s_xt = sem("b_xt_copied")
        s_gp = sem("b_gate_product")
        s_g = sem("b_gate_copied")
        s_sort = sem("b_sort_chain")
        s_idx = sem("b_index_parts")
        s_cast = sem("b_index_cast")
        s_nmax = sem("b_negative_max")
        s_exp = sem("b_exponentials")
        s_rt = sem("b_reciprocal_totals")
        s_wt = sem("b_gate_softmax")
        s_bp = sem("b_index_broadcast")
        s_dist = sem("b_distance")
        s_hot = sem("b_one_hot")
        s_mask = sem("b_pool_mask")
        s_cp = sem("b_candidates")
        s_cs = sem("b_candidates_copied")
        s_kept = sem("b_kept")
        s_acc = sem("b_accumulated")
        s_gx = sem("b_gathered_weighted")
        s_tp = sem("b_gathered_transposed")
        s_ts = sem("b_gathered_transpose_copied")
        s_xsp = sem("b_shared_x_transposed")
        s_xss = sem("b_shared_x_copied")
        s_h = sem("b_hidden")
        s_si = sem("b_silu")
        s_a = sem("b_activated")
        s_dn = sem("b_down")
        s_st = sem("b_stats")
        s_mv = sem("b_moments")
        s_sd = sem("b_deviation")
        s_rs = sem("b_reciprocal")
        s_yn = sem("b_normed")
        s_np = sem("b_normed_transposed")
        s_ns = sem("b_normed_scaled")
        s_mp = sem("b_mlp_hidden")
        s_ms = sem("b_mlp_silu")
        s_op = sem("b_mlp_out")
        s_o = sem("b_result")
        s_out = sem("b_stored")

        loads = [
            (w_gu[:], t["w_gu"]), (w_dn[:], t["w_dn"]), (ws_gu[:], t["ws_gu"]), (ws_dn[:], t["ws_dn"]),
            (m1[:], t["m1"]), (m2[:], t["m2"]), (m2b[:], t["m2b"]), (cols[:], t["cols"]), (ident[:], t["ident"]),
            (pick[:], t["pick"]), (gather[:], t["gather"]), (minus_slot[:], t["minus_slot"]),
        ]
        N_W = 16 * len(loads)

        def steps(engine, body):
            body(0, 0)
            body(1, 1)
            with engine.Fori(2, TILES - 1, 2) as k:
                body(k, 0)
                body(k + 1, 1)
            body(TILES - 1, 0)
            body(TILES, 1)
        assert TILES % 2 == 1

        with ExitStack() as setup:
            pos_w = cand[0][0:HALF, 0:2 * D]
            posT = cand[1][0:HALF + 1, 0:2 * E]
            pos_b = cand[2][0:1, 0:D]
            raw_w = kept[0][0:HALF, 0:2 * D]
            pe_l = kept[1][0:E, 0:D]
            pe_t = kept[2][0:HALF, 0:2 * E]
            with nc.Block() as block:
                @block.sync
                def _(sp):
                    for dst, src in loads:
                        sp.dma_start(dst, src).then_inc(s_w, 16)
                    sp.dma_start(pos_w, t["pos_w"]).then_inc(s_pe, 16)
                    sp.dma_start(posT[0:HALF, :], t["posT"]).then_inc(s_pe, 16)
                    sp.dma_start(pos_b, t["pos_b"]).then_inc(s_pe, 16)
                    sp.dma_start(raw_w, t["gate_w"]).then_inc(s_pe, 16)
                    for e in range(E):
                        sp.dma_start(gatew[HALF:HALF + 1, 1, e * D:(e + 1) * D], t["gate_b"]).then_inc(s_pe, 16)
                    sp.wait_ge(s_w, N_W)

                @block.gpsimd
                def _(pool):
                    nc.gpsimd.memset(xbd[:], 0.0)

                @block.vector
                def _(dve):
                    nc.vector.memset(eps[:], 1e-6)
                    nc.vector.memset(ones[:], 1.0)
                    nc.vector.memset(xt[HALF:HALF + 1, :, :], 1.0).then_inc(s_const, 1)
                    dve.wait_ge(s_pet, 1)
                    nc.vector.reduce_max(nmax[0:E, 0:1], p_misc[0:E, 0:D], mybir.AxisListType.X).then_inc(s_pet, 1)
                    dve.wait_ge(s_pet, 2)
                    nc.vector.tensor_scalar(nmax[0:E, 1:2], nmax[0:E, 0:1], -1.0, None, ALU.mult).then_inc(s_pet, 1)
                    dve.wait_ge(s_pet, 4)
                    nc.vector.reciprocal(rtotal[0:E, 0:1], total[0:E, 0:1]).then_inc(s_pet, 1)
                    dve.wait_ge(s_pet, 5)
                    nc.vector.tensor_scalar(pe_l, pe_l, rtotal[0:E, 0:1], None, ALU.mult).then_inc(s_pet, 1)
                    dve.wait_ge(s_pet, 7)
                    nc.vector.tensor_copy(pe_t, p_misc[0:HALF, 0:2 * E]).then_inc(s_pet, 1)
                    dve.wait_ge(s_pet, 8)
                    for e in range(E):
                        for f in range(2):
                            op = nc.vector.tensor_scalar(gatew[0:HALF, f, e * D:(e + 1) * D],
                                                         raw_w[:, f * D:(f + 1) * D],
                                                         pe_t[:, f * E + e:f * E + e + 1], None, ALU.mult)
                    op.then_inc(s_gw0, 1)

                @block.scalar
                def _(act):
                    act.wait_ge(s_pet, 3)
                    nc.scalar.activation(pe_l, p_misc[0:E, 0:D], ACT.Exp, bias=nmax[0:E, 1:2],
                                         accum_out=total[0:E, 0:1]).then_inc(s_pet, 1)

                @block.tensor
                def _(pe):
                    pe.wait_ge(s_w, N_W)
                    pe.wait_ge(s_pe, 16 * (4 + E))
                    pe.wait_ge(s_const, 1)
                    for f in range(2):
                        nc.tensor.matmul(p_misc[0:E, 0:D], posT[0:HALF, f * E:(f + 1) * E],
                                         pos_w[:, f * D:(f + 1) * D], start=f == 0, stop=False)
                    nc.tensor.matmul(p_misc[0:E, 0:D], ones[:, 0:E], pos_b, start=False, stop=True)\
                        .then_inc(s_pet, 1)
                    pe.wait_ge(s_pet, 6)
                    for f in range(2):
                        mm = nc.tensor.transpose(p_misc[0:HALF, f * E:(f + 1) * E],
                                                 pe_l[:, f * HALF:(f + 1) * HALF], ident[0:E, 0:E])
                    mm.then_inc(s_pet, 1)

        def is_first(k):
            return isinstance(k, int) and k == 0

        def is_last(k):
            return isinstance(k, int) and k == TILES

        with nc.Block() as block:
            @block.sync
            def _(sp):
                sp.dma_start(xin[:], x2_dram[0:128]).then_inc(s_xin, 16)

                def load_diagonal(tile, k):
                    wait(sp, s_cp, UNITS * (k - 1))
                    sp.sem_inc(s_held_sp, 1)
                    for m in range(SPLIT):
                        rows = parts_dram[m, bass.ds(128 * tile, 128)].rearrange(
                            "(g t) (h l) -> t h g l", t=GROUP, l=LO)
                        for b in range(GROUP):
                            sp.dma_start(xbd[b * LO:b * LO + HI, m, :, b, :], rows[b]).then_inc(s_bd, 16)

                def body(k, parity):
                    n = k - 1
                    if not is_last(k):
                        sp.wait_ge(s_xtp, k + 1)
                        sp.sem_inc(s_held_sp, 1)
                        sp.dma_start(xin[:], x2_dram[bass.ds(128 * (k + 1), 128)] if not is_first(k)
                                     else x2_dram[128:256]).then_inc(s_xin, 16)
                    if not is_first(k):
                        wait(sp, s_xsp, n)
                        sp.sem_inc(s_held_sp, 1)
                        sp.dma_start(xsh[:], x2_dram[bass.ds(128 * n, 128)]).then_inc(s_xsh, 16)
                        wait(sp, s_o, n)
                        sp.dma_start(h1t[:], h1_dram[bass.ds(128 * n, 128)]).then_inc(s_h1, 16)
                    if not is_last(k):
                        load_diagonal(k, k + 1)
                    if not is_first(k):
                        sp.wait_ge(s_o, k)
                        sp.dma_start(out[bass.ds(128 * n, 128)], res[:]).then_inc(s_out, 16)
                steps(sp, body)
                sp.wait_ge(s_out, 16 * TILES)

            @block.tensor
            def _(pe):
                def transposes(k):
                    pe.wait_ge(s_xin, 16 * (k + 2))
                    wait(pe, s_ns, k - 1)
                    wait(pe, s_g, GATES * (k + 1))
                    wait(pe, s_o, k - 1)
                    for f in range(2):
                        mm = nc.tensor.transpose(p_misc[0:HALF, f * 128:(f + 1) * 128],
                                                 xin[:, f * HALF:(f + 1) * HALF], ident[:])
                    mm.then_inc(s_xtp, 1)

                def gates(k, q):
                    if q == 0:
                        pe.wait_ge(s_xt, k + 2)
                    else:
                        pe.wait_ge(s_g, GATES * (k + 1) + q)
                    for f in range(2):
                        mm = nc.tensor.matmul(p_misc[:, 0:2 * D], xt[0:HALF + f, f, :],
                                              gatew[0:HALF + f, f, 2 * q * D:2 * (q + 1) * D],
                                              start=f == 0, stop=f == 1)
                    mm.then_inc(s_gp, 1)

                def broadcast(k, u):
                    done = UNITS * (k - 1)
                    at = slice((u % PARTS) * WIDE, (u % PARTS + 1) * WIDE)
                    if u == 0:
                        pe.wait_ge(s_cast, 2 * k)
                        wait(pe, s_a, BLOCKS * (k - 1))
                    wait(pe, s_dist, done + u)
                    nc.tensor.matmul(pair[:, 0, :], pick[:, u // PARTS, :], hi[:, at], start=True, stop=True)
                    nc.tensor.matmul(pair[:, 1, :], pick[:, u // PARTS, :], lo[:, at], start=True, stop=True)\
                        .then_inc(s_bp, 1)

                def candidates(k, u):
                    done = UNITS * (k - 1)
                    if u == 0:
                        pe.wait_ge(s_bd, 16 * SPLIT * GROUP * k)
                    if u < 2:
                        wait(pe, s_yn, k - 1)
                        wait(pe, s_ts, E // 4 * (k - 1))
                    wait(pe, s_cs, done + u - 1)
                    pe.wait_ge(s_hot, done + u + 1)
                    for m in range(SPLIT):
                        mm = nc.tensor.matmul(p_cand[:, u % 2, :],
                                              xbd[:, m, u // PARTS].rearrange("p a b -> p (a b)"),
                                              marks[u % RING][:, 0, :], start=m == 0, stop=m == SPLIT - 1)
                    mm.then_inc(s_cp, 1)

                def accumulate(k, u):
                    done = UNITS * (k - 1)
                    grp = u // PARTS
                    if u == 0:
                        wait(pe, s_gx, PARTS * (k - 1))
                    pe.wait_ge(s_kept, done + u + 1)
                    first = 128 - GROUP - GROUP * grp
                    nc.tensor.matmul(acc[:, u % PARTS, :], gather[:, first:first + 128], kept[u % RING][:],
                                     start=grp == 0, stop=grp == GROUPS - 1,
                                     skip_group_check=True).then_inc(s_acc, 1)

                def shared_transposes(k):
                    pe.wait_ge(s_xsh, 16 * k)
                    wait(pe, s_g, GATES * (k + 1) if is_last(k) else GATES * (k + 2))
                    for f in range(2):
                        mm = nc.tensor.transpose(p_misc[0:HALF, f * 128:(f + 1) * 128],
                                                 xsh[:, f * HALF:(f + 1) * HALF], ident[:])
                    mm.then_inc(s_xsp, 1)

                def expert_transposes(k, q):
                    if q == 0:
                        pe.wait_ge(s_gx, PARTS * k)
                    pe.wait_ge(s_cs, UNITS * k)
                    wait(pe, s_ts, E // 4 * (k - 1) + q)
                    for j in range(4):
                        mm = nc.tensor.transpose(p_t[0:K, j * 128:(j + 1) * 128], w[1 - parity_of[0]][:, 4 * q + j, :],
                                                 ident[:])
                    mm.then_inc(s_tp, 1)

                def hidden(k, b):
                    if b < 2:
                        pe.wait_ge(s_dist, UNITS * k)
                    wait(pe, s_a, BLOCKS * (k - 1) + b - 1)
                    dst = pair[:, b % 2]
                    if b < SHARED:
                        pe.wait_ge(s_xss, k)
                        for m in range(4):
                            col = (m // 2) * SI + b * D + (m % 2) * HALF
                            for f in range(2):
                                mm = nc.tensor.matmul(dst[0:HALF, m * 128:(m + 1) * 128],
                                                      ws_gu[:, f, col:col + HALF], xst[:, f, :],
                                                      start=f == 0, stop=f == 1)
                    else:
                        e = b - SHARED
                        pe.wait_ge(s_ts, E // 4 * (k - 1) + e // 4 + 1)
                        for m in range(4):
                            mm = nc.tensor.matmul(dst[0:HALF, m * 128:(m + 1) * 128],
                                                  w_gu[:, e, m * HALF:(m + 1) * HALF], gwt[(e // 4) % 2][:, e % 4, :],
                                                  start=True, stop=True)
                    mm.then_inc(s_h, 1)

                def down(k, b):
                    if b == 0:
                        pe.wait_ge(s_cs, UNITS * k)
                    pe.wait_ge(s_a, BLOCKS * (k - 1) + b + 1)
                    for f in range(2):
                        wd = ws_dn[:, b, f, :] if b < SHARED else w_dn[:, b - SHARED, f, :]
                        mm = nc.tensor.matmul(p_y[:, 0:D], act_s[b % 2][:, f * 128:(f + 1) * 128], wd,
                                              start=b == 0 and f == 0, stop=b == BLOCKS - 1 and f == 1)
                    mm.then_inc(s_dn, 1)

                def tail(k):
                    pe.wait_ge(s_xss, k)
                    pe.wait_ge(s_yn, k)
                    for f in range(2):
                        mm = nc.tensor.transpose(p_misc[0:HALF, f * 128:(f + 1) * 128],
                                                 yn[:, f * HALF:(f + 1) * HALF], ident[:])
                    mm.then_inc(s_np, 1)
                    pe.wait_ge(s_ns, k)
                    for m in range(2):
                        for f in range(2):
                            mm = nc.tensor.matmul(p_misc[0:HALF, 256 + m * 128:256 + (m + 1) * 128],
                                                  m1[:, f, m * HALF:(m + 1) * HALF], ynt[:, f, :],
                                                  start=f == 0, stop=f == 1)
                    mm.then_inc(s_mp, 1)
                    pe.wait_ge(s_ms, k)
                    for f in range(2):
                        nc.tensor.matmul(p_misc[:, 0:D], mid[:, f, :], m2[:, f, :], start=f == 0, stop=False)
                    nc.tensor.matmul(p_misc[:, 0:D], ones[:, :], m2b[:, :], start=False, stop=True)\
                        .then_inc(s_op, 1)

                parity_of = [0]

                def body(k, parity):
                    parity_of[0] = parity
                    if not is_last(k):
                        transposes(k)
                    if is_first(k):
                        for q in range(GATES):
                            gates(k, q)
                        return
                    for u in range(UNITS + LAG):
                        if u < UNITS:
                            broadcast(k, u)
                        if 1 <= u < UNITS + 1:
                            candidates(k, u - 1)
                        if u >= LAG:
                            accumulate(k, u - LAG)
                        if u % 5 == 4 and u // 5 < GATES and not is_last(k):
                            gates(k, u // 5)
                    shared_transposes(k)
                    for b in range(BLOCKS + 1):
                        if b == SHARED:
                            expert_transposes(k, 0)
                        if b < BLOCKS:
                            hidden(k, b)
                        if b >= 1:
                            down(k, b - 1)
                        if b >= SHARED and (b - SHARED) % 4 == 0 and (b - SHARED) // 4 + 1 < E // 4:
                            expert_transposes(k, (b - SHARED) // 4 + 1)
                    tail(k)

                transposes(-1)
                for q in range(GATES):
                    gates(-1, q)
                steps(pe, body)

            @block.scalar
            def _(act):
                def copy_xt(k):
                    act.wait_ge(s_xtp, k + 2)
                    wait(act, s_gp, GATES * (k + 1))
                    nc.scalar.activation(xt[0:HALF].rearrange("p a b -> p (a b)"), p_misc[0:HALF, 0:256],
                                         ACT.Copy).then_inc(s_xt, 1)

                def copy_gates(k, q, parity):
                    act.wait_ge(s_gp, GATES * (k + 1) + q + 1)
                    nc.scalar.activation(g[1 - parity][:, 2 * q:2 * q + 2, :].rearrange("p a b -> p (a b)"),
                                         p_misc[:, 0:2 * D], ACT.Copy).then_inc(s_g, 1)

                def distance(k, u):
                    act.wait_ge(s_bp, UNITS * (k - 1) + u + 1)
                    if (u - RING) % 2:
                        wait(act, s_mask, masks(k, u - RING))
                    nc.scalar.activation(dist[u % RING][:], pair[:], ACT.Abs, bias=minus_slot[:]).then_inc(s_dist, 1)

                def mark(k, u):
                    act.wait_ge(s_dist, UNITS * (k - 1) + u + 1)
                    wait(act, s_cp, UNITS * (k - 1) + u + 1 - RING)
                    wait(act, s_kept, UNITS * (k - 1) + u + 1 - RING)
                    n = 1 if u % 2 else 2
                    nc.scalar.activation(marks[u % RING][:, 0:n], dist[u % RING][:, 0:n], ACT.Relu, bias=1.0,
                                         scale=-1.0).then_inc(s_hot, 1)

                def copy_candidates(k, u):
                    act.wait_ge(s_cp, UNITS * (k - 1) + u + 1)
                    wait(act, s_kept, UNITS * (k - 1) + u + 1 - RING)
                    nc.scalar.activation(cand[u % RING][:], p_cand[:, u % 2, :], ACT.Copy).then_inc(s_cs, 1)

                def body(k, parity):
                    p = 1 - parity
                    if not is_first(k):
                        act.wait_ge(s_idx, 2 * k)
                        nc.scalar.activation(hi[:], hi[:].bitcast(U16), ACT.Copy).then_inc(s_cast, 1)
                        nc.scalar.activation(lo[:], lo[:].bitcast(U16), ACT.Copy).then_inc(s_cast, 1)
                    if not is_last(k):
                        copy_xt(k)
                    if is_first(k):
                        for q in range(GATES):
                            copy_gates(k, q, parity)
                        return
                    for u in range(UNITS + 1):
                        if u < UNITS:
                            distance(k, u)
                            mark(k, u)
                        if u:
                            copy_candidates(k, u - 1)
                        if u == 5:
                            act.wait_ge(s_nmax, k)
                            for e in range(E):
                                op = nc.scalar.activation(w[p][:, e, :], w[p][:, e, :], ACT.Exp,
                                                          bias=nmax[:, e:e + 1], accum_out=total[:, e:e + 1])
                            op.then_inc(s_exp, 1)
                        if u % 5 == 4 and u // 5 < GATES and not is_last(k):
                            copy_gates(k, u // 5, parity)
                    act.wait_ge(s_xsp, k)
                    nc.scalar.activation(xst[:].rearrange("p a b -> p (a b)"), p_misc[0:HALF, 0:256],
                                         ACT.Copy).then_inc(s_xss, 1)
                    def copy_t(q):
                        act.wait_ge(s_tp, E // 4 * (k - 1) + q + 1)
                        if q >= 2:
                            act.wait_ge(s_h, BLOCKS * (k - 1) + SHARED + 4 * (q - 1))
                        nc.scalar.activation(gwt[q % 2][:].rearrange("p a b -> p (a b)"), p_t[0:K, :],
                                             ACT.Copy).then_inc(s_ts, 1)
                    for b in range(BLOCKS):
                        if b == SHARED:
                            copy_t(0)
                        act.wait_ge(s_h, BLOCKS * (k - 1) + b + 1)
                        wait(act, s_a, BLOCKS * (k - 1) + b - 1)
                        nc.scalar.activation(silu[b % 2][:], pair[0:HALF, b % 2, 0:256], ACT.Silu).then_inc(s_si, 1)
                        if b >= SHARED and (b - SHARED) % 4 == 0 and (b - SHARED) // 4 + 1 < E // 4:
                            copy_t((b - SHARED) // 4 + 1)
                    act.wait_ge(s_mv, k)
                    nc.scalar.activation(sd[:], mv[:, 1:2], ACT.Sqrt, bias=eps[:]).then_inc(s_sd, 1)
                    act.wait_ge(s_np, k)
                    for f in range(2):
                        op = nc.scalar.activation(ynt[:, f, :], p_misc[0:HALF, f * 128:(f + 1) * 128], ACT.Identity,
                                                  scale=cols[:, f:f + 1], bias=cols[:, 2 + f:3 + f])
                    op.then_inc(s_ns, 1)
                    act.wait_ge(s_mp, k)
                    for f in range(2):
                        op = nc.scalar.activation(mid[:, f, :], p_misc[0:HALF, 256 + f * 128:256 + (f + 1) * 128],
                                                  ACT.Silu, bias=cols[:, 4 + f:5 + f])
                    op.then_inc(s_ms, 1)

                copy_xt(-1)
                for q in range(GATES):
                    copy_gates(-1, q, 1)
                steps(act, body)

            @block.gpsimd
            def _(pool):
                def body(k, parity):
                    if is_first(k):
                        return
                    done = UNITS * (k - 1)

                    def mask(u):
                        pool.wait_ge(s_dist, done + u + 1)
                        pool.sem_inc(s_held, 1)
                        nc.gpsimd.tensor_scalar(marks[u % RING][:, 1, :], dist[u % RING][:, 1, :], 0.0, None,
                                                ALU.is_equal).then_inc(s_mask, 1)

                    def keep(u):
                        wait(pool, s_acc, done + u + 1 - RING)
                        if u % 2:
                            pool.wait_ge(s_mask, masks(k, u))
                        else:
                            pool.wait_ge(s_hot, done + u + 1)
                        pool.wait_ge(s_cs, done + u + 1)
                        nc.gpsimd.tensor_tensor(kept[u % RING][:], marks[u % RING][:, 1, :], cand[u % RING][:],
                                                ALU.mult).then_inc(s_kept, 1)
                    for u in range(UNITS + 1):
                        if u < UNITS and u % 2:
                            mask(u)
                        if u:
                            keep(u - 1)
                steps(pool, body)

            @block.vector
            def _(dve):
                def start(k, parity):
                    p = 1 - parity
                    dve.wait_ge(s_sort, SORT_INCS)
                    dve.sem_clear(s_sort)
                    wait(dve, s_bp, UNITS * (k - 1))
                    flat = idx[:].rearrange("p a b -> p (a b)")
                    nc.vector.tensor_scalar(hi[:].bitcast(U16), flat, 4, None,
                                            ALU.logical_shift_right).then_inc(s_idx, 1)
                    nc.vector.tensor_scalar(lo[:].bitcast(U16), flat, LO - 1, None,
                                            ALU.bitwise_and).then_inc(s_idx, 1)
                    nc.vector.tensor_scalar(nmax[:], w[p][:, :, 0], -1.0, None, ALU.mult).then_inc(s_nmax, 1)

                def normalise(k, p):
                    dve.wait_ge(s_exp, k)
                    nc.vector.reciprocal(rtotal[:], total[:]).then_inc(s_rt, 1)
                    dve.wait_ge(s_rt, k)
                    nc.vector.tensor_tensor(w[p][:], w[p][:], rtotal[:].unsqueeze(2).to_broadcast([128, E, K]),
                                            ALU.mult).then_inc(s_wt, 1)

                def weigh(k, p, c):
                    if c == 0:
                        dve.wait_ge(s_wt, k)
                        dve.wait_ge(s_acc, UNITS * k)
                    flat = w[p][:].rearrange("p a b -> p (a b)")[:, c * WIDE:(c + 1) * WIDE]
                    nc.vector.tensor_tensor(flat, acc[:, c, :], flat, ALU.mult).then_inc(s_gx, 1)

                def activate(k, b):
                    dve.wait_ge(s_si, BLOCKS * (k - 1) + b + 1)
                    wait(dve, s_dn, BLOCKS * (k - 1) + b - 1)
                    nc.vector.tensor_tensor(act_s[b % 2][:], silu[b % 2][:], pair[0:HALF, b % 2, 256:512],
                                            ALU.mult).then_inc(s_a, 1)

                def norm_stats(k):
                    dve.wait_ge(s_dn, BLOCKS * k)
                    nc.vector.bn_stats(stats[:], p_y[:, 0:D]).then_inc(s_st, 1)

                def norm_moments(k):
                    dve.wait_ge(s_st, k)
                    dve.sem_inc(s_held_v, 1)
                    nc.vector.bn_aggr(mv[:], stats[:]).then_inc(s_mv, 1)

                def norm_reciprocal(k):
                    dve.wait_ge(s_sd, k)
                    nc.vector.reciprocal(rstd[:], sd[:]).then_inc(s_rs, 1)

                def norm_apply(k):
                    dve.wait_ge(s_rs, k)
                    nc.vector.tensor_scalar(yn[:], p_y[:, 0:D], mv[:, 0:1], rstd[:, 0:1], ALU.subtract,
                                            ALU.mult).then_inc(s_yn, 1)

                def residual(k):
                    dve.wait_ge(s_h1, 16 * k)
                    wait(dve, s_out, 16 * (k - 1))
                    dve.wait_ge(s_op, k)
                    nc.vector.tensor_tensor(res[:], p_misc[:, 0:D], h1t[:], ALU.add).then_inc(s_o, 1)

                def body(k, parity):
                    p = 1 - parity
                    if not is_first(k):
                        start(k, parity)
                    if not is_last(k):
                        wait(dve, s_tp, E // 4 * (k - 1))
                        dve.wait_ge(s_g, GATES * (k + 1))
                        nc.vector.tensor_copy(carrier[:], eps[:])
                    incs = 0
                    for step in range(ROUNDS * E // 2):
                        pair, r = step // ROUNDS, step % ROUNDS
                        if not is_last(k):
                            feats = [g[parity][:, 2 * pair + i, :] for i in range(2)]
                            tops = [w[parity][:, 2 * pair + i, 8 * r:8 * r + 8] for i in range(2)]
                            for i in range(2):
                                if r:
                                    dve.wait_ge(s_sort, incs - 1)
                                nc.vector.max(tops[i], feats[i]).then_inc(s_sort, 1)
                                incs += 1
                            for i in range(2):
                                dve.wait_ge(s_sort, incs - 1 + i)
                                nc.vector.max_index(idx[:, 2 * pair + i, 8 * r:8 * r + 8], tops[i], feats[i])
                            for i in range(2):
                                nc.vector.match_replace(feats[i], tops[i], feats[i], LOWEST).then_inc(s_sort, 1)
                                incs += 1
                        if is_first(k):
                            continue
                        if step == 8:
                            normalise(k, p)
                        if step == WEIGH:
                            for c in range(PARTS):
                                weigh(k, p, c)
                        if WEIGH < step <= WEIGH + BLOCKS:
                            activate(k, step - WEIGH - 1)
                        if step == WEIGH + 20:
                            norm_stats(k)
                            norm_moments(k)
                        if step == WEIGH + 21:
                            norm_reciprocal(k)
                            norm_apply(k)
                        if step == WEIGH + 24:
                            residual(k)
                steps(dve, body)


def build(nc, t, out):
    h1_dram = nc.dram_tensor("h1_scratch", [PADDED, D], F32, kind="Internal").ap()
    x2_dram = nc.dram_tensor("x2_scratch", [PADDED, D], F32, kind="Internal").ap()
    parts_dram = nc.dram_tensor("parts_scratch", [SPLIT, PADDED, D], BF16, kind="Internal").ap()
    phase_a(nc, t, h1_dram, x2_dram, parts_dram)
    phase_b(nc, t, h1_dram, x2_dram, parts_dram, out)


def kernel(**inputs):
    import ml_dtypes
    import numpy as np
    import concourse.bacc as bacc
    from concourse.bass_utils import run_bass_kernel_spmd

    a = {n.replace("L0_", "").replace("ffn_", "").replace("attn_", ""): np.asarray(v) for n, v in inputs.items()}

    def chunked(m, p=HALF):
        return m.reshape(-1, p, m.shape[-1]).transpose(1, 0, 2)

    x = a["x"].reshape(IMAGES, CHANNELS, SIDE, PATCH, SIDE, PATCH).transpose(0, 1, 3, 5, 2, 4)
    x = x.reshape(IMAGES, PC, 128, SIDE * SIDE).transpose(0, 2, 1, 3)
    patches = np.zeros((IMAGES, 128, PC, TOKENS), x.dtype)
    patches[..., 1:] = x
    base = np.zeros((2 * CHUNK[0], D), x.dtype)
    base[:] = a["tok_b_lin"]
    base[0] = a["tok_cls_token"][0]
    wkv = np.zeros((2, HALF + 1, 2 * D), x.dtype)
    wkv[:, :HALF] = np.concatenate([a["Wk"].T, a["Wv"].T], axis=1).reshape(2, HALF, 2 * D)
    wkv[1, HALF] = np.concatenate([a["bk"], a["bv"]])
    tok = np.arange(128)
    pick = (tok[:, None] == np.repeat(tok, LO)[None, :]).reshape(128, GROUPS, GROUP * LO)
    gather = (np.arange(2 * 128 - GROUP)[None, :] - (128 - GROUP)) == (np.arange(GROUP * LO) // LO)[:, None]
    t = {
        "patches": patches,
        "w_lin": a["tok_W_lin"].T,
        "base": base.reshape(2, CHUNK[0], D),
        "wq": a["Wq"].T,
        "bq": a["bq"].reshape(2, HALF).T,
        "wkv": wkv,
        "ident": np.eye(128, dtype=np.float32),
        "pos_w": chunked(a["pos_w"]).reshape(HALF, 2 * D),
        "posT": chunked(a["posembed"].T).reshape(HALF, 2 * E),
        "pos_b": a["pos_b"][None],
        "gate_w": chunked(a["gate_w"]).reshape(HALF, 2 * D),
        "gate_b": a["gate_b"][None],
        "w_gu": np.concatenate([a["eg_w"], a["eu_w"]], axis=2).transpose(1, 0, 2),
        "w_dn": a["ed_w"].reshape(E, 2, HALF, D).transpose(2, 0, 1, 3),
        "ws_gu": chunked(np.concatenate([a["sg_w"], a["su_w"]], axis=1)),
        "ws_dn": a["sd_w"].reshape(SHARED, 2, HALF, D).transpose(2, 0, 1, 3),
        "m1": chunked(a["m1_w"]),
        "m2": chunked(a["m2_w"]),
        "m2b": a["m2_b"][None],
        "cols": np.concatenate([a[n].reshape(2, HALF) for n in ("ln_g", "ln_b", "m1_b")]).T,
        "pick": pick.astype(ml_dtypes.bfloat16),
        "gather": gather.astype(np.float32),
        "minus_slot": -(tok % LO).astype(np.float32)[:, None],
    }
    nc = bacc.Bacc("TRN2", target_bir_lowering=False, num_devices=1)
    arrays, aps = {}, {}
    for name, value in t.items():
        value = np.ascontiguousarray(value)
        arrays[f"in_{name}"] = value
        aps[name] = nc.dram_tensor(f"in_{name}", value.shape, mybir.dt.from_np(value.dtype),
                                   kind="ExternalInput").ap()
    out = nc.dram_tensor("out_rows", [TILES * 128, D], F32, kind="ExternalOutput").ap()
    build(nc, aps, out)
    result = run_bass_kernel_spmd(nc, [arrays], core_ids=[0]).results[0]["out_rows"]
    return result[:ROWS].reshape(IMAGES, TOKENS, D)
```

```python
from contextlib import ExitStack

import concourse.bass as bass
from concourse import mybir

ALU = mybir.AluOpType
ACT = mybir.ActivationFunctionType
F32 = mybir.dt.float32
BF16 = mybir.dt.bfloat16
U16 = mybir.dt.uint16

IMAGES, SIDE, PATCH, CHANNELS = 64, 14, 16, 3
TOKENS = SIDE * SIDE + 1
PATCH_DIM = CHANNELS * PATCH * PATCH
PC = PATCH_DIM // 128
D = 192
HALF = D // 2
CHUNK = [99, 98]
E = 16
K = D // 2
SI = 2 * D
ROUNDS = K // 8
ROWS = IMAGES * TOKENS
TILES = -(-ROWS // 128)
PADDED = (TILES + 1) * 128
LO, HI = 16, D // 16
GROUP = 8
GROUPS = 128 // GROUP
WIDE = 512
PARTS = E * K // WIDE
UNITS = GROUPS * PARTS
RING = 4
LAG = 3
SHARED = SI // D
BLOCKS = E + SHARED
GATES = E // 2
LOWEST = -3.0e38
BATCH = 4
EARLY = SHARED + 2 * BATCH

X_ROUND, EXP_ROUND, SHARED_ROUND = 0, 2, 20
GATE_ROUNDS = [4, 8, 12, 16, 30, 33, 36, 40]
BATCH_ROUNDS = [22, 38, 1, 2]
NORM_ROUND, MLP1_ROUND, MLP2_ROUND = 25, 26, 28
SQRT_ROUND = 20
BLOCK_ROUNDS = [23, 25] + [27, 29, 31, 33] + [41, 43, 45, 47] + [3 + 2 * j for j in range(E - 2 * BATCH)]
DOWN_LAG = 3
MISC = sorted([(X_ROUND, "x", 0), (SHARED_ROUND, "shared", 0), (NORM_ROUND, "norm", 0), (MLP1_ROUND, "mlp1", 0),
               (MLP2_ROUND, "mlp2", 0)] + [(r, "gate", q) for q, r in enumerate(GATE_ROUNDS)]
              + [(r, "batch", q) for q, r in enumerate(BATCH_ROUNDS)])


NORMALISE_STEP = 14


def sort_step(r):
    return 12 * r // 7 + (11 if r <= SHARED_ROUND else 12)


WEIGH_STEPS = [41, 70, 95]


def exists(k, use):
    if not isinstance(k, int):
        return True
    name, q = use[1:]
    if name in ("x", "gate"):
        return k < TILES
    if name == "shared" or (name == "batch" and q < 2):
        return 1 <= k <= TILES
    return k >= 2
SORT_INCS = 2 * 2 * ROUNDS * (E // 2)
PER_STEP = 4
STEPS_A = IMAGES // PER_STEP
SPLIT = 3


def wait(engine, semaphore, value):
    if isinstance(value, int) and value <= 0:
        return
    engine.wait_ge(semaphore, value)


def masks(k, u):
    return UNITS // 2 * (k - 1) + (u + 1) // 2


def phase_a(nc, t, h1_dram, x2_dram, parts_dram):
    with ExitStack() as ctx:
        def sb(name, shape, dt=F32):
            return ctx.enter_context(nc.sbuf_tensor(name, shape, dt))

        def sem(name):
            return ctx.enter_context(nc.semaphore(name))

        n_img = PER_STEP
        wlin = sb("wlin", [128, PC, D])
        base = sb("base", [CHUNK[0], 2, D])
        wq = sb("wq", [HALF, 2, D])
        bq = sb("bq", [HALF, 2])
        wkv = sb("wkv", [HALF + 1, 2, 2 * D])
        ident = sb("ident_a", [128, 128])
        eps = sb("eps_a", [128, 1])
        zeros = sb("zeros", [128, D])
        patches = [sb(f"patches{i}", [128, PC, TOKENS]) for i in range(n_img)]
        h0 = [sb(f"h0_{i}", [CHUNK[0], 2, D]) for i in range(n_img)]
        stats = [sb(f"stats{i}", [CHUNK[0], 2, 6]) for i in range(n_img)]
        mv = [sb(f"mv{i}", [CHUNK[0], 2, 2]) for i in range(n_img)]
        sd = [sb(f"sd{i}", [CHUNK[0], 2]) for i in range(n_img)]
        rstd = [sb(f"rstd{i}", [CHUNK[0], 2]) for i in range(n_img)]
        xn = [sb(f"xn{i}", [CHUNK[0], 2, D]) for i in range(n_img)]
        xnt = [sb(f"xnt{i}", [HALF + 1, 2, TOKENS]) for i in range(n_img)]
        qt = [sb(f"qt{i}", [HALF, 2, TOKENS]) for i in range(n_img)]
        kv = [sb(f"kv{i}", [CHUNK[0], 2, 2 * D]) for i in range(n_img)]
        kvm = [sb(f"kvm{i}", [HALF, 2, D]) for i in range(n_img)]
        h1 = [sb(f"h1_{i}", [CHUNK[0], 2, D]) for i in range(n_img)]
        x2 = [sb(f"x2_{i}", [CHUNK[0], 2, D]) for i in range(n_img)]
        parts = [sb(f"parts{i}", [CHUNK[0], SPLIT, 2, D], BF16) for i in range(n_img)]
        rest = [sb(f"rest{i}", [CHUNK[0], 2, D]) for i in range(n_img)]
        pa = [ctx.enter_context(nc.psum_tensor(f"pa{i}", [128, WIDE], F32)) for i in range(n_img)]
        pb = [ctx.enter_context(nc.psum_tensor(f"pb{i}", [128, WIDE], F32)) for i in range(n_img)]

        s_w = sem("a_weights")
        s_zero = sem("a_zeros")
        s_eps = sem("a_eps")
        s_held = sem("a_vector_waits_passed")
        s_ones = sem("a_ones_row")
        s_in = [sem(f"a_patches_loaded{i}") for i in range(n_img)]
        s_emb = sem("a_embedded")
        s_h0 = sem("a_h0")
        s_st = sem("a_stats")
        s_mv = sem("a_moments")
        s_sd = sem("a_deviation")
        s_rs = sem("a_reciprocal")
        s_xn = sem("a_normed")
        s_xtp = sem("a_transposed")
        s_xt = sem("a_transpose_copied")
        s_q = sem("a_q_product")
        s_qt = sem("a_q_copied")
        s_kvp = sem("a_kv_product")
        s_kv = sem("a_kv_copied")
        s_mp = sem("a_memory_product")
        s_m = sem("a_memory_copied")
        s_op = sem("a_attended")
        s_h1 = sem("a_h1")
        s_st2 = sem("a_stats2")
        s_mv2 = sem("a_moments2")
        s_sd2 = sem("a_deviation2")
        s_rs2 = sem("a_reciprocal2")
        s_x2 = sem("a_normed2")
        s_part = sem("a_parts")
        s_pad = sem("a_padding_stored")
        s_out = sem("a_stored")
        N_W = 6 * 16

        def steps(engine, body):
            body(0)
            with engine.Fori(1, STEPS_A - 1) as it:
                body(it)
            body(STEPS_A - 1)

        with nc.Block() as block:
            @block.sync
            def _(sp):
                sp.dma_start(wlin[:], t["w_lin"].rearrange("(c p) n -> p c n", p=128)).then_inc(s_w, 16)
                sp.dma_start(base[:], t["base"].rearrange("c p n -> p c n")).then_inc(s_w, 16)
                sp.dma_start(wq[:], t["wq"].rearrange("(c p) n -> p c n", p=HALF)).then_inc(s_w, 16)
                sp.dma_start(bq[:], t["bq"]).then_inc(s_w, 16)
                sp.dma_start(wkv[:], t["wkv"].rearrange("c p n -> p c n")).then_inc(s_w, 16)
                sp.dma_start(ident[:], t["ident"]).then_inc(s_w, 16)

                def load(it):
                    for i in range(n_img):
                        wait(sp, s_emb, n_img * (it - 1) + i + 1)
                        sp.dma_start(patches[i][:], t["patches"][bass.ds(n_img * it + i, 1)]
                                     .rearrange("a p c n -> (a p) c n")).then_inc(s_in[i], 16)

                sp.wait_ge(s_zero, 1)
                for first in range(ROWS, PADDED, 64):
                    sp.dma_start(h1_dram[first:first + 64], zeros[0:64, :]).then_inc(s_pad, 16)
                    sp.dma_start(x2_dram[first:first + 64], zeros[0:64, :]).then_inc(s_pad, 16)
                    for m in range(SPLIT):
                        sp.dma_start(parts_dram[m, first:first + 64], zeros[0:64, 0:HALF].bitcast(BF16))\
                            .then_inc(s_pad, 16)
                sp.wait_ge(s_pad, 16 * (2 + SPLIT) * (PADDED - ROWS) // 64)
                load(0)

                def body(it):
                    if not isinstance(it, int) or it < STEPS_A - 1:
                        load(it + 1)
                    for i in range(n_img):
                        row = TOKENS * (n_img * it + i)
                        sp.wait_ge(s_part, 4 * (n_img * it + i + 1))
                        for c, size in enumerate(CHUNK):
                            rows = bass.ds(row + c * CHUNK[0], size)
                            sp.dma_start(h1_dram[rows], h1[i][0:size, c, :]).then_inc(s_out, 16)
                            sp.dma_start(x2_dram[rows], x2[i][0:size, c, :]).then_inc(s_out, 16)
                            sp.dma_start(parts_dram[:, rows].rearrange("m p n -> p m n"),
                                         parts[i][0:size, :, c, :]).then_inc(s_out, 16)
                steps(sp, body)
                sp.wait_ge(s_out, 16 * 6 * IMAGES)

            @block.gpsimd
            def _(pool):
                nc.gpsimd.memset(zeros[:], 0.0).then_inc(s_zero, 1)

                def body(it):
                    for i in range(n_img):
                        pool.wait_ge(s_x2, n_img * it + i + 1)
                        seen = 4 * (n_img * it + i)
                        for c, size in enumerate(CHUNK):
                            op = nc.gpsimd.tensor_tensor(parts[i][0:size, 0, c, :], x2[i][0:size, c, :],
                                                         zeros[0:size, :], ALU.add)
                        op.then_inc(s_part, 1)
                        pool.wait_ge(s_part, seen + 1)
                        for c, size in enumerate(CHUNK):
                            op = nc.gpsimd.tensor_tensor(rest[i][0:size, c, :], x2[i][0:size, c, :],
                                                         parts[i][0:size, 0, c, :], ALU.subtract)
                        op.then_inc(s_part, 1)
                        pool.wait_ge(s_part, seen + 2)
                        for c, size in enumerate(CHUNK):
                            op = nc.gpsimd.tensor_tensor(parts[i][0:size, 1, c, :], rest[i][0:size, c, :],
                                                         zeros[0:size, :], ALU.add)
                        op.then_inc(s_part, 1)
                        pool.wait_ge(s_part, seen + 3)
                        for c, size in enumerate(CHUNK):
                            op = nc.gpsimd.tensor_tensor(parts[i][0:size, 2, c, :], rest[i][0:size, c, :],
                                                         parts[i][0:size, 1, c, :], ALU.subtract)
                        op.then_inc(s_part, 1)
                steps(pool, body)

            @block.tensor
            def _(pe):
                pe.wait_ge(s_w, N_W)

                def body(it):
                    def n(i):
                        return n_img * it + i + 1
                    for i in range(n_img):
                        wait(pe, s_qt, n(i) - n_img)
                        wait(pe, s_kv, 2 * (n(i) - n_img))
                        pe.wait_ge(s_in[i], 16 * (it + 1))
                        for c, size in enumerate(CHUNK):
                            for p in range(PC):
                                mm = nc.tensor.matmul(pa[i][0:size, c * D:(c + 1) * D],
                                                      patches[i][:, p, c * CHUNK[0]:c * CHUNK[0] + size],
                                                      wlin[:, p, :], start=p == 0, stop=p == PC - 1)
                        mm.then_inc(s_emb, 1)
                    for i in range(n_img):
                        wait(pe, s_h1, n(i) - n_img)
                        pe.wait_ge(s_xn, n(i))
                        for f in range(2):
                            for c, size in enumerate(CHUNK):
                                at = f * TOKENS + c * CHUNK[0]
                                mm = nc.tensor.transpose(pb[i][0:HALF, at:at + size],
                                                         xn[i][0:size, c, f * HALF:(f + 1) * HALF],
                                                         ident[0:size, 0:size])
                        mm.then_inc(s_xtp, 1)
                    for i in range(n_img):
                        pe.wait_ge(s_h0, n(i))
                        pe.wait_ge(s_ones, 1)
                        pe.wait_ge(s_xt, n(i))
                        for e in range(2):
                            for f in range(2):
                                mm = nc.tensor.matmul(pa[i][0:HALF, e * TOKENS:(e + 1) * TOKENS],
                                                      wq[:, f, e * HALF:(e + 1) * HALF], xnt[i][0:HALF, f, :],
                                                      start=f == 0, stop=f == 1)
                        mm.then_inc(s_q, 1)
                    for i in range(n_img):
                        for c, size in enumerate(CHUNK):
                            if c:
                                pe.wait_ge(s_qt, n(i))
                            out = (pb, pa)[c][i]
                            for f in range(2):
                                mm = nc.tensor.matmul(out[0:size, 0:2 * D],
                                                      xnt[i][0:HALF + f, f, c * CHUNK[0]:c * CHUNK[0] + size],
                                                      wkv[0:HALF + f, f, :], start=f == 0, stop=f == 1)
                            mm.then_inc(s_kvp, 1)
                    for i in range(n_img):
                        pe.wait_ge(s_kv, 2 * n(i))
                        for f in range(2):
                            for c, size in enumerate(CHUNK):
                                mm = nc.tensor.matmul(pb[i][0:HALF, f * D:(f + 1) * D],
                                                      kv[i][0:size, c, f * HALF:(f + 1) * HALF],
                                                      kv[i][0:size, c, D:2 * D], start=c == 0, stop=c == 1)
                        mm.then_inc(s_mp, 1)
                    for i in range(n_img):
                        pe.wait_ge(s_m, n(i))
                        for c, size in enumerate(CHUNK):
                            for f in range(2):
                                mm = nc.tensor.matmul(pb[i][0:size, c * D:(c + 1) * D],
                                                      qt[i][:, f, c * CHUNK[0]:c * CHUNK[0] + size],
                                                      kvm[i][:, f, :], start=f == 0, stop=f == 1)
                        mm.then_inc(s_op, 1)
                steps(pe, body)

            @block.vector
            def _(dve):
                nc.vector.memset(eps[:], 1e-5).then_inc(s_eps, 1)
                for i in range(n_img):
                    op = nc.vector.memset(xnt[i][HALF:HALF + 1, :, :], 1.0)
                op.then_inc(s_ones, 1)
                dve.wait_ge(s_w, N_W)

                def norm(it, src, dst, s_src, s_stat, s_mom, s_dev, s_rec, s_dst):
                    def n(i):
                        return n_img * it + i + 1
                    for i in range(n_img):
                        dve.wait_ge(s_src, n(i))
                        wait(dve, s_dst, n(i) - n_img)
                        for c, size in enumerate(CHUNK):
                            op = nc.vector.bn_stats(stats[i][0:size, c, :], src[i][0:size, c, :])
                        op.then_inc(s_stat, 1)
                    for i in range(n_img):
                        dve.wait_ge(s_stat, n(i))
                        dve.sem_inc(s_held, 1)
                        for c, size in enumerate(CHUNK):
                            op = nc.vector.bn_aggr(mv[i][0:size, c, :], stats[i][0:size, c, :])
                        op.then_inc(s_mom, 1)
                    for i in range(n_img):
                        dve.wait_ge(s_dev, n(i))
                        for c, size in enumerate(CHUNK):
                            op = nc.vector.reciprocal(rstd[i][0:size, c:c + 1], sd[i][0:size, c:c + 1])
                        op.then_inc(s_rec, 1)
                    for i in range(n_img):
                        dve.wait_ge(s_rec, n(i))
                        for c, size in enumerate(CHUNK):
                            op = nc.vector.tensor_scalar(dst[i][0:size, c, :], src[i][0:size, c, :],
                                                         mv[i][0:size, c, 0:1], rstd[i][0:size, c:c + 1],
                                                         ALU.subtract, ALU.mult)
                        op.then_inc(s_dst, 1)

                def body(it):
                    def n(i):
                        return n_img * it + i + 1
                    for i in range(n_img):
                        dve.wait_ge(s_emb, n(i))
                        for c, size in enumerate(CHUNK):
                            op = nc.vector.tensor_tensor(h0[i][0:size, c, :], pa[i][0:size, c * D:(c + 1) * D],
                                                         base[0:size, c, :], ALU.add)
                        op.then_inc(s_h0, 1)
                    norm(it, h0, xn, s_h0, s_st, s_mv, s_sd, s_rs, s_xn)
                    for i in range(n_img):
                        for c, size in enumerate(CHUNK):
                            dve.wait_ge(s_kvp, 2 * (n(i) - 1) + c + 1)
                            nc.vector.tensor_copy(kv[i][0:size, c, :], (pb, pa)[c][i][0:size, 0:2 * D])\
                                .then_inc(s_kv, 1)
                    for i in range(n_img):
                        if i == 0 and not (isinstance(it, int) and it == 0):
                            dve.wait_ge(s_out, 16 * 6 * n_img * it)
                        dve.wait_ge(s_op, n(i))
                        for c, size in enumerate(CHUNK):
                            op = nc.vector.tensor_tensor(h1[i][0:size, c, :], pb[i][0:size, c * D:(c + 1) * D],
                                                         h0[i][0:size, c, :], ALU.add)
                        op.then_inc(s_h1, 1)
                    norm(it, h1, x2, s_h1, s_st2, s_mv2, s_sd2, s_rs2, s_x2)
                steps(dve, body)

            @block.scalar
            def _(act):
                act.wait_ge(s_eps, 1)
                act.wait_ge(s_w, N_W)

                def body(it):
                    def n(i):
                        return n_img * it + i + 1
                    for i in range(n_img):
                        act.wait_ge(s_mv, n(i))
                        for c, size in enumerate(CHUNK):
                            op = nc.scalar.activation(sd[i][0:size, c:c + 1], mv[i][0:size, c, 1:2], ACT.Sqrt,
                                                      bias=eps[0:size, :])
                        op.then_inc(s_sd, 1)
                    for i in range(n_img):
                        act.wait_ge(s_xtp, n(i))
                        nc.scalar.activation(xnt[i][0:HALF, :, :].rearrange("p a b -> p (a b)"),
                                             pb[i][0:HALF, 0:2 * TOKENS], ACT.Copy).then_inc(s_xt, 1)
                    for i in range(n_img):
                        act.wait_ge(s_q, n(i))
                        for e in range(2):
                            op = nc.scalar.activation(qt[i][:, e, :], pa[i][0:HALF, e * TOKENS:(e + 1) * TOKENS],
                                                      ACT.Identity, bias=bq[:, e:e + 1])
                        op.then_inc(s_qt, 1)
                    for i in range(n_img):
                        act.wait_ge(s_mp, n(i))
                        nc.scalar.activation(kvm[i][:].rearrange("p a b -> p (a b)"), pb[i][0:HALF, 0:2 * D],
                                             ACT.Copy, scale=float(D) ** -0.5).then_inc(s_m, 1)
                    for i in range(n_img):
                        act.wait_ge(s_mv2, n(i))
                        for c, size in enumerate(CHUNK):
                            op = nc.scalar.activation(sd[i][0:size, c:c + 1], mv[i][0:size, c, 1:2], ACT.Sqrt,
                                                      bias=eps[0:size, :])
                        op.then_inc(s_sd2, 1)
                steps(act, body)


def phase_b(nc, t, h1_dram, x2_dram, parts_dram, out):
    with ExitStack() as ctx:
        def sb(name, shape, dt=F32):
            return ctx.enter_context(nc.sbuf_tensor(name, shape, dt))

        def sem(name):
            return ctx.enter_context(nc.semaphore(name))

        gatew = sb("gatew", [HALF + 1, 2, E * D])
        w_gu = sb("w_gu", [K, E, 2 * D])
        w_dn = sb("w_dn", [HALF, E, 2, D])
        ws_gu = sb("ws_gu", [HALF, 2, 2 * SI])
        ws_dn = sb("ws_dn", [HALF, SHARED, 2, D])
        m1 = sb("m1", [HALF, 2, D])
        m2 = sb("m2", [HALF, 2, D])
        m2b = sb("m2b", [1, D])
        cols = sb("cols", [HALF, 6])
        ident = sb("ident_b", [128, 128])
        pick = sb("pick", [128, GROUPS, 128], BF16)
        gather = sb("gather", [128, 2 * 128 - GROUP])
        minus_slot = sb("minus_slot", [128, 1])
        ones = sb("ones", [1, 128])
        eps = sb("eps_b", [128, 1])
        xin = sb("xin", [128, D])
        xsh = sb("xsh", [128, D])
        h1t = sb("h1t", [128, D])
        xt = sb("xt", [HALF + 1, 2, 128])
        xst = sb("xst", [HALF, 2, 128])
        g = [sb(f"g{b}", [128, E, D]) for b in range(2)]
        w = [sb(f"w{b}", [128, E, K]) for b in range(2)]
        idx = sb("idx", [128, E, K], U16)
        hi = sb("hi", [128, E * K], BF16)
        lo = sb("lo", [128, E * K], BF16)
        nmax = sb("nmax", [128, E])
        total = sb("total", [128, E])
        rtotal = sb("rtotal", [128, E])
        xbd = [sb(f"xbd{b}", [128, SPLIT, GROUPS, GROUP, LO], BF16) for b in range(2)]
        dist = [sb(f"dist{r}", [128, 2, WIDE], BF16) for r in range(RING)]
        marks = [sb(f"marks{r}", [128, 2, WIDE], BF16) for r in range(RING)]
        cand = [sb(f"cand{r}", [128, WIDE]) for r in range(RING)]
        kept = [sb(f"kept{r}", [128, WIDE]) for r in range(RING)]
        gwt = [sb(f"gwt{b}", [K, 4, 128]) for b in range(2)]
        silu = sb("silu", [HALF, 2 * 128])
        act_s = [sb(f"act{b}", [HALF, 2 * 128]) for b in range(2)]
        carrier = sb("carrier", [128, 1])
        stats = sb("stats_b", [128, 6])
        mv = sb("mv_b", [128, 2])
        sd = sb("sd_b", [128, 1])
        rstd = sb("rstd_b", [128, 1])
        yn = sb("yn", [128, D])
        ynt = sb("ynt", [HALF, 2, 128])
        mid = sb("mid", [HALF, 2, 128])
        res = sb("res", [128, D])

        def bank(name, n=1):
            return ctx.enter_context(nc.psum_tensor(name, [128, n, WIDE], F32))
        acc = bank("acc")[:, 0]
        pair = bank("pair", 2)
        p_cand = bank("p_cand", 2)
        p_h = bank("p_h")[:, 0]
        p_y = bank("p_y")[:, 0]
        p_misc = bank("p_misc")[:, 0]

        s_w = sem("b_weights")
        s_const = sem("b_constants")
        s_held = sem("b_pool_waits_passed")
        s_held_v = sem("b_vector_waits_passed")
        s_held_sp = sem("b_load_waits_passed")
        s_pe = sem("b_posembed")
        s_pet = sem("b_posembed_steps")
        s_gw0 = sem("b_gate_weights")
        s_xin = sem("b_x_loaded")
        s_xsh = sem("b_shared_x_loaded")
        s_h1 = sem("b_h1_loaded")
        s_bd = sem("b_block_diagonal_loaded")
        s_xtp = sem("b_x_transposed")
        s_xt = sem("b_xt_copied")
        s_gp = sem("b_gate_product")
        s_g = sem("b_gate_copied")
        s_sort = sem("b_sort_chain")
        s_idx = sem("b_index_parts")
        s_cast = sem("b_index_cast")
        s_nmax = sem("b_negative_max")
        s_exp = sem("b_exponentials")
        s_rt = sem("b_reciprocal_totals")
        s_wt = sem("b_gate_softmax")
        s_bp = sem("b_index_broadcast")
        s_dist = sem("b_distance")
        s_hot = sem("b_one_hot")
        s_mask = sem("b_pool_mask")
        s_cp = sem("b_candidates")
        s_cs = sem("b_candidates_copied")
        s_kept = sem("b_kept")
        s_acc = sem("b_accumulated")
        s_gx = sem("b_gathered_weighted")
        s_tp = sem("b_gathered_transposed")
        s_ts = sem("b_gathered_transpose_copied")
        s_xsp = sem("b_shared_x_transposed")
        s_xss = sem("b_shared_x_copied")
        s_h = sem("b_hidden")
        s_si = sem("b_silu")
        s_a = sem("b_activated")
        s_dn = sem("b_down")
        s_st = sem("b_stats")
        s_mv = sem("b_moments")
        s_sd = sem("b_deviation")
        s_rs = sem("b_reciprocal")
        s_yn = sem("b_normed")
        s_np = sem("b_normed_transposed")
        s_ns = sem("b_normed_scaled")
        s_mp = sem("b_mlp_hidden")
        s_ms = sem("b_mlp_silu")
        s_op = sem("b_mlp_out")
        s_o = sem("b_result")
        s_out = sem("b_stored")

        loads = [
            (w_gu[:], t["w_gu"]), (w_dn[:], t["w_dn"]), (ws_gu[:], t["ws_gu"]), (ws_dn[:], t["ws_dn"]),
            (m1[:], t["m1"]), (m2[:], t["m2"]), (m2b[:], t["m2b"]), (cols[:], t["cols"]), (ident[:], t["ident"]),
            (pick[:], t["pick"]), (gather[:], t["gather"]), (minus_slot[:], t["minus_slot"]),
        ]
        N_W = 16 * len(loads)

        def steps(engine, body):
            for k in range(3):
                body(k, k % 2)
            with engine.Fori(3, TILES - 1, 2) as k:
                body(k, 1)
                body(k + 1, 0)
            body(TILES, TILES % 2)
            body(TILES + 1, (TILES + 1) % 2)
        assert TILES % 2 == 1

        with ExitStack():
            pos_w = cand[0][0:HALF, 0:2 * D]
            posT = cand[1][0:HALF + 1, 0:2 * E]
            pos_b = cand[2][0:1, 0:D]
            raw_w = kept[0][0:HALF, 0:2 * D]
            pe_l = kept[1][0:E, 0:D]
            pe_t = kept[2][0:HALF, 0:2 * E]
            with nc.Block() as block:
                @block.sync
                def _(sp):
                    for dst, src in loads:
                        sp.dma_start(dst, src).then_inc(s_w, 16)
                    sp.dma_start(pos_w, t["pos_w"]).then_inc(s_pe, 16)
                    sp.dma_start(posT[0:HALF, :], t["posT"]).then_inc(s_pe, 16)
                    sp.dma_start(pos_b, t["pos_b"]).then_inc(s_pe, 16)
                    sp.dma_start(raw_w, t["gate_w"]).then_inc(s_pe, 16)
                    for e in range(E):
                        sp.dma_start(gatew[HALF:HALF + 1, 1, e * D:(e + 1) * D], t["gate_b"]).then_inc(s_pe, 16)
                    sp.wait_ge(s_w, N_W)

                @block.gpsimd
                def _(pool):
                    for b in range(2):
                        nc.gpsimd.memset(xbd[b][:], 0.0)

                @block.vector
                def _(dve):
                    nc.vector.memset(eps[:], 1e-6)
                    nc.vector.memset(ones[:], 1.0)
                    nc.vector.memset(xt[HALF:HALF + 1, :, :], 1.0).then_inc(s_const, 1)
                    dve.wait_ge(s_pet, 1)
                    nc.vector.reduce_max(nmax[0:E, 0:1], p_misc[0:E, 0:D], mybir.AxisListType.X).then_inc(s_pet, 1)
                    dve.wait_ge(s_pet, 2)
                    nc.vector.tensor_scalar(nmax[0:E, 1:2], nmax[0:E, 0:1], -1.0, None, ALU.mult).then_inc(s_pet, 1)
                    dve.wait_ge(s_pet, 4)
                    nc.vector.reciprocal(rtotal[0:E, 0:1], total[0:E, 0:1]).then_inc(s_pet, 1)
                    dve.wait_ge(s_pet, 5)
                    nc.vector.tensor_scalar(pe_l, pe_l, rtotal[0:E, 0:1], None, ALU.mult).then_inc(s_pet, 1)
                    dve.wait_ge(s_pet, 7)
                    nc.vector.tensor_copy(pe_t, p_misc[0:HALF, 0:2 * E]).then_inc(s_pet, 1)
                    dve.wait_ge(s_pet, 8)
                    for e in range(E):
                        for f in range(2):
                            op = nc.vector.tensor_scalar(gatew[0:HALF, f, e * D:(e + 1) * D],
                                                         raw_w[:, f * D:(f + 1) * D],
                                                         pe_t[:, f * E + e:f * E + e + 1], None, ALU.mult)
                    op.then_inc(s_gw0, 1)

                @block.scalar
                def _(act):
                    act.wait_ge(s_pet, 3)
                    nc.scalar.activation(pe_l, p_misc[0:E, 0:D], ACT.Exp, bias=nmax[0:E, 1:2],
                                         accum_out=total[0:E, 0:1]).then_inc(s_pet, 1)

                @block.tensor
                def _(pe):
                    pe.wait_ge(s_w, N_W)
                    pe.wait_ge(s_pe, 16 * (4 + E))
                    pe.wait_ge(s_const, 1)
                    for f in range(2):
                        nc.tensor.matmul(p_misc[0:E, 0:D], posT[0:HALF, f * E:(f + 1) * E],
                                         pos_w[:, f * D:(f + 1) * D], start=f == 0, stop=False)
                    nc.tensor.matmul(p_misc[0:E, 0:D], ones[:, 0:E], pos_b, start=False, stop=True)\
                        .then_inc(s_pet, 1)
                    pe.wait_ge(s_pet, 6)
                    for f in range(2):
                        mm = nc.tensor.transpose(p_misc[0:HALF, f * E:(f + 1) * E],
                                                 pe_l[:, f * HALF:(f + 1) * HALF], ident[0:E, 0:E])
                    mm.then_inc(s_pet, 1)

        def sorts(k):
            return not isinstance(k, int) or k < TILES

        def gathers(k):
            return not isinstance(k, int) or 1 <= k <= TILES

        def finishes(k):
            return not isinstance(k, int) or k >= 2

        def copied(k, use):
            name, q = use[1:]
            if name == "x":
                return s_xt, k + 2
            if name == "gate":
                return s_g, GATES * (k + 1) + q + 1
            if name == "shared":
                return s_xss, k
            if name == "batch":
                return s_ts, E // BATCH * (k - 1 - q // 2) + q + 1
            return {"norm": s_ns, "mlp1": s_ms, "mlp2": s_o}[name], k - 1

        def block_count(k, b):
            return BLOCKS * (k - 1 - (b >= EARLY)) + b + 1

        def blocks_at(k, r, lag=0):
            return [b for b in range(BLOCKS) if BLOCK_ROUNDS[b] + lag == r
                    and (gathers(k) if b < EARLY else finishes(k))]

        with nc.Block() as block:
            @block.sync
            def _(sp):
                sp.dma_start(xin[:], x2_dram[0:128]).then_inc(s_xin, 16)

                def load_diagonal(k, parity):
                    wait(sp, s_cp, UNITS * (k - 1))
                    sp.sem_inc(s_held_sp, 1)
                    for m in range(SPLIT):
                        rows = parts_dram[m, bass.ds(128 * k, 128)].rearrange(
                            "(g t) (h l) -> t h g l", t=GROUP, l=LO)
                        for b in range(GROUP):
                            sp.dma_start(xbd[parity][b * LO:b * LO + HI, m, :, b, :], rows[b]).then_inc(s_bd, 16)

                def body(k, parity):
                    if sorts(k):
                        sp.wait_ge(s_xtp, k + 1)
                        sp.sem_inc(s_held_sp, 1)
                        sp.dma_start(xin[:], x2_dram[bass.ds(128 * (k + 1), 128)]).then_inc(s_xin, 16)
                        wait(sp, s_bd, 16 * SPLIT * GROUP * k)
                        sp.sem_inc(s_held_sp, 1)
                        load_diagonal(k, parity)
                    if gathers(k):
                        wait(sp, s_xsp, k - 1)
                        sp.sem_inc(s_held_sp, 1)
                        sp.dma_start(xsh[:], x2_dram[bass.ds(128 * (k - 1), 128)]).then_inc(s_xsh, 16)
                    if finishes(k):
                        wait(sp, s_o, k - 2)
                        sp.sem_inc(s_held_sp, 1)
                        sp.dma_start(h1t[:], h1_dram[bass.ds(128 * (k - 2), 128)]).then_inc(s_h1, 16)
                        sp.wait_ge(s_o, k - 1)
                        sp.sem_inc(s_held_sp, 1)
                        sp.dma_start(out[bass.ds(128 * (k - 2), 128)], res[:]).then_inc(s_out, 16)
                steps(sp, body)
                sp.wait_ge(s_out, 16 * TILES)

            @block.tensor
            def _(pe):
                def claim(k, name, q=0):
                    uses = [(j, u) for j in (k - 1, k) for u in MISC if exists(j, u)]
                    here = [i for i, (j, u) in enumerate(uses) if j is k and u[1:] == (name, q)][0]
                    if here:
                        wait(pe, *copied(*uses[here - 1]))

                def transposes(k, first=False):
                    if not first:
                        claim(k, "x")
                    pe.wait_ge(s_xin, 16 * (k + 2))
                    for f in range(2):
                        mm = nc.tensor.transpose(p_misc[0:HALF, f * 128:(f + 1) * 128],
                                                 xin[:, f * HALF:(f + 1) * HALF], ident[:])
                    mm.then_inc(s_xtp, 1)

                def gates(k, q, first=False):
                    if first:
                        wait(pe, s_g, q)
                    else:
                        claim(k, "gate", q)
                    if q == 0:
                        pe.wait_ge(s_xt, k + 2)
                    for f in range(2):
                        mm = nc.tensor.matmul(p_misc[:, 0:2 * D], xt[0:HALF + f, f, :],
                                              gatew[0:HALF + f, f, 2 * q * D:2 * (q + 1) * D],
                                              start=f == 0, stop=f == 1)
                    mm.then_inc(s_gp, 1)

                def broadcast(k, u):
                    at = slice(u // GROUPS * WIDE, (u // GROUPS + 1) * WIDE)
                    if u == 0:
                        pe.wait_ge(s_cast, 2 * k)
                    wait(pe, s_dist, UNITS * (k - 1) + u)
                    nc.tensor.matmul(pair[:, 0, :], pick[:, u % GROUPS, :], hi[:, at], start=True, stop=True)
                    nc.tensor.matmul(pair[:, 1, :], pick[:, u % GROUPS, :], lo[:, at], start=True, stop=True)\
                        .then_inc(s_bp, 1)

                def candidates(k, u, parity):
                    done = UNITS * (k - 1)
                    if u == 0:
                        pe.wait_ge(s_bd, 16 * SPLIT * GROUP * k)
                    wait(pe, s_cs, done + u - 1)
                    pe.wait_ge(s_hot, done + u + 1)
                    for m in range(SPLIT):
                        mm = nc.tensor.matmul(p_cand[:, u % 2, :],
                                              xbd[1 - parity][:, m, u % GROUPS].rearrange("p a b -> p (a b)"),
                                              marks[u % RING][:, 0, :], start=m == 0, stop=m == SPLIT - 1)
                    mm.then_inc(s_cp, 1)

                def accumulate(k, u):
                    grp = u % GROUPS
                    if grp == 0:
                        wait(pe, s_gx, PARTS * (k - 1) + u // GROUPS)
                    pe.wait_ge(s_kept, UNITS * (k - 1) + u + 1)
                    first = 128 - GROUP - GROUP * grp
                    nc.tensor.matmul(acc[:, :], gather[:, first:first + 128], kept[u % RING][:],
                                     start=grp == 0, stop=grp == GROUPS - 1).then_inc(s_acc, 1)

                def shared_transposes(k):
                    claim(k, "shared")
                    pe.wait_ge(s_xsh, 16 * k)
                    for f in range(2):
                        mm = nc.tensor.transpose(p_misc[0:HALF, f * 128:(f + 1) * 128],
                                                 xsh[:, f * HALF:(f + 1) * HALF], ident[:])
                    mm.then_inc(s_xsp, 1)

                def batch(k, q, parity):
                    claim(k, "batch", q)
                    pe.wait_ge(s_gx, PARTS * (k - 1) + q + 1 if q < 2 else PARTS * (k - 1))
                    src = w[1 - parity] if q < 2 else w[parity]
                    for j in range(BATCH):
                        mm = nc.tensor.transpose(p_misc[0:K, j * 128:(j + 1) * 128], src[:, BATCH * q + j, :], ident[:])
                    mm.then_inc(s_tp, 1)

                def hidden(k, b):
                    wait(pe, s_a, block_count(k, b) - 1)
                    if b < SHARED:
                        pe.wait_ge(s_xss, k)
                        for m in range(4):
                            col = (m // 2) * SI + b * D + (m % 2) * HALF
                            for f in range(2):
                                mm = nc.tensor.matmul(p_h[0:HALF, m * 128:(m + 1) * 128],
                                                      ws_gu[:, f, col:col + HALF], xst[:, f, :],
                                                      start=f == 0, stop=f == 1)
                    else:
                        e = b - SHARED
                        pe.wait_ge(s_ts, E // BATCH * (k - 1 - (b >= EARLY)) + e // BATCH + 1)
                        for m in range(4):
                            mm = nc.tensor.matmul(p_h[0:HALF, m * 128:(m + 1) * 128],
                                                  w_gu[:, e, m * HALF:(m + 1) * HALF],
                                                  gwt[(e // BATCH) % 2][:, e % BATCH, :], start=True, stop=True)
                    mm.then_inc(s_h, 1)

                def down(k, b):
                    if b == 0:
                        wait(pe, s_yn, k - 1)
                    pe.wait_ge(s_a, block_count(k, b))
                    for f in range(2):
                        wd = ws_dn[:, b, f, :] if b < SHARED else w_dn[:, b - SHARED, f, :]
                        mm = nc.tensor.matmul(p_y[:, 0:D], act_s[b % 2][:, f * 128:(f + 1) * 128], wd,
                                              start=b == 0 and f == 0, stop=b == BLOCKS - 1 and f == 1)
                    mm.then_inc(s_dn, 1)

                def norm_transposes(k):
                    claim(k, "norm")
                    pe.wait_ge(s_yn, k - 1)
                    for f in range(2):
                        mm = nc.tensor.transpose(p_misc[0:HALF, f * 128:(f + 1) * 128],
                                                 yn[:, f * HALF:(f + 1) * HALF], ident[:])
                    mm.then_inc(s_np, 1)

                def mlp1(k):
                    claim(k, "mlp1")
                    for m in range(2):
                        for f in range(2):
                            mm = nc.tensor.matmul(p_misc[0:HALF, m * 128:(m + 1) * 128],
                                                  m1[:, f, m * HALF:(m + 1) * HALF], ynt[:, f, :],
                                                  start=f == 0, stop=f == 1)
                    mm.then_inc(s_mp, 1)

                def mlp2(k):
                    claim(k, "mlp2")
                    for f in range(2):
                        nc.tensor.matmul(p_misc[:, 0:D], mid[:, f, :], m2[:, f, :], start=f == 0, stop=False)
                    nc.tensor.matmul(p_misc[:, 0:D], ones[:, :], m2b[:, :], start=False, stop=True)\
                        .then_inc(s_op, 1)

                def body(k, parity):
                    for r in range(UNITS + LAG):
                        if gathers(k):
                            if r < UNITS:
                                broadcast(k, r)
                            if 1 <= r < UNITS + 1:
                                candidates(k, r - 1, parity)
                            if r >= LAG:
                                accumulate(k, r - LAG)
                        for b in blocks_at(k, r, DOWN_LAG):
                            down(k, b)
                        for b in blocks_at(k, r):
                            hidden(k, b)
                        if sorts(k):
                            if r == X_ROUND:
                                transposes(k)
                            if r in GATE_ROUNDS:
                                gates(k, GATE_ROUNDS.index(r))
                        if gathers(k):
                            if r == SHARED_ROUND:
                                shared_transposes(k)
                            if r in BATCH_ROUNDS[:2]:
                                batch(k, BATCH_ROUNDS.index(r), parity)
                        if finishes(k):
                            if r in BATCH_ROUNDS[2:]:
                                batch(k, BATCH_ROUNDS.index(r), parity)
                            if r == NORM_ROUND:
                                norm_transposes(k)
                            if r == MLP1_ROUND:
                                mlp1(k)
                            if r == MLP2_ROUND:
                                mlp2(k)

                transposes(-1, first=True)
                for q in range(GATES):
                    gates(-1, q, first=True)
                steps(pe, body)

            @block.scalar
            def _(act):
                def copy_xt(k):
                    act.wait_ge(s_xtp, k + 2)
                    wait(act, s_gp, GATES * (k + 1))
                    nc.scalar.activation(xt[0:HALF].rearrange("p a b -> p (a b)"), p_misc[0:HALF, 0:256],
                                         ACT.Copy).then_inc(s_xt, 1)

                def copy_gates(k, q, parity):
                    act.wait_ge(s_gp, GATES * (k + 1) + q + 1)
                    nc.scalar.activation(g[1 - parity][:, 2 * q:2 * q + 2, :].rearrange("p a b -> p (a b)"),
                                         p_misc[:, 0:2 * D], ACT.Copy).then_inc(s_g, 1)

                def distance(k, u):
                    act.wait_ge(s_bp, UNITS * (k - 1) + u + 1)
                    if (u - RING) % 2:
                        wait(act, s_mask, masks(k, u - RING))
                    nc.scalar.activation(dist[u % RING][:], pair[:], ACT.Abs, bias=minus_slot[:]).then_inc(s_dist, 1)

                def mark(k, u):
                    act.wait_ge(s_dist, UNITS * (k - 1) + u + 1)
                    wait(act, s_cp, UNITS * (k - 1) + u + 1 - RING)
                    wait(act, s_kept, UNITS * (k - 1) + u + 1 - RING)
                    n = 1 if u % 2 else 2
                    nc.scalar.activation(marks[u % RING][:, 0:n], dist[u % RING][:, 0:n], ACT.Relu, bias=1.0,
                                         scale=-1.0).then_inc(s_hot, 1)

                def copy_candidates(k, u):
                    act.wait_ge(s_cp, UNITS * (k - 1) + u + 1)
                    wait(act, s_kept, UNITS * (k - 1) + u + 1 - RING)
                    nc.scalar.activation(cand[u % RING][:], p_cand[:, u % 2, :], ACT.Copy).then_inc(s_cs, 1)

                def copy_batch(k, q):
                    count = E // BATCH * (k - 1 - q // 2) + q + 1
                    act.wait_ge(s_tp, count)
                    wait(act, s_h, BLOCKS * (k - 1 - q // 2) + SHARED + BATCH * (q - 1) if q >= 2 else
                         BLOCKS * (k - 2) + SHARED + BATCH * (q + 3))
                    nc.scalar.activation(gwt[q % 2][:].rearrange("p a b -> p (a b)"), p_misc[0:K, :],
                                         ACT.Copy).then_inc(s_ts, 1)

                def body(k, parity):
                    p = 1 - parity
                    if gathers(k):
                        act.wait_ge(s_idx, 2 * k)
                        nc.scalar.activation(hi[:], hi[:].bitcast(U16), ACT.Copy).then_inc(s_cast, 1)
                        nc.scalar.activation(lo[:], lo[:].bitcast(U16), ACT.Copy).then_inc(s_cast, 1)
                    for r in range(UNITS + 1):
                        if gathers(k):
                            if r < UNITS:
                                distance(k, r)
                            if r:
                                copy_candidates(k, r - 1)
                            if r < UNITS:
                                mark(k, r)
                            if r == EXP_ROUND:
                                act.wait_ge(s_nmax, k)
                                for e in range(E):
                                    op = nc.scalar.activation(w[p][:, e, :], w[p][:, e, :], ACT.Exp,
                                                              bias=nmax[:, e:e + 1], accum_out=total[:, e:e + 1])
                                op.then_inc(s_exp, 1)
                        for b in blocks_at(k, r):
                            act.wait_ge(s_h, block_count(k, b))
                            wait(act, s_a, block_count(k, b) - 1)
                            nc.scalar.activation(silu[:], p_h[0:HALF, 0:256], ACT.Silu).then_inc(s_si, 1)
                        if sorts(k):
                            if r == X_ROUND:
                                copy_xt(k)
                            if r in GATE_ROUNDS:
                                copy_gates(k, GATE_ROUNDS.index(r), parity)
                        if gathers(k):
                            if r == SHARED_ROUND:
                                act.wait_ge(s_xsp, k)
                                wait(act, s_h, BLOCKS * (k - 2) + SHARED)
                                nc.scalar.activation(xst[:].rearrange("p a b -> p (a b)"), p_misc[0:HALF, 0:256],
                                                     ACT.Copy).then_inc(s_xss, 1)
                            if r in BATCH_ROUNDS[:2]:
                                copy_batch(k, BATCH_ROUNDS.index(r))
                        if finishes(k):
                            if r in BATCH_ROUNDS[2:]:
                                copy_batch(k, BATCH_ROUNDS.index(r))
                            if r == SQRT_ROUND + 1:
                                act.wait_ge(s_mv, k - 1)
                                nc.scalar.activation(sd[:], mv[:, 1:2], ACT.Sqrt, bias=eps[:]).then_inc(s_sd, 1)
                            if r == NORM_ROUND:
                                act.wait_ge(s_np, k - 1)
                                for f in range(2):
                                    op = nc.scalar.activation(ynt[:, f, :], p_misc[0:HALF, f * 128:(f + 1) * 128],
                                                              ACT.Identity, scale=cols[:, f:f + 1],
                                                              bias=cols[:, 2 + f:3 + f])
                                op.then_inc(s_ns, 1)
                            if r == MLP1_ROUND:
                                act.wait_ge(s_mp, k - 1)
                                for f in range(2):
                                    op = nc.scalar.activation(mid[:, f, :], p_misc[0:HALF, f * 128:(f + 1) * 128],
                                                              ACT.Silu, bias=cols[:, 4 + f:5 + f])
                                op.then_inc(s_ms, 1)

                copy_xt(-1)
                for q in range(GATES):
                    copy_gates(-1, q, 1)
                steps(act, body)

            @block.gpsimd
            def _(pool):
                def body(k, parity):
                    if not gathers(k):
                        return
                    done = UNITS * (k - 1)

                    def mask(u):
                        pool.wait_ge(s_dist, done + u + 1)
                        pool.sem_inc(s_held, 1)
                        nc.gpsimd.tensor_scalar(marks[u % RING][:, 1, :], dist[u % RING][:, 1, :], 0.0, None,
                                                ALU.is_equal).then_inc(s_mask, 1)

                    def keep(u):
                        wait(pool, s_acc, done + u + 1 - RING)
                        if u % 2:
                            pool.wait_ge(s_mask, masks(k, u))
                        else:
                            pool.wait_ge(s_hot, done + u + 1)
                        pool.wait_ge(s_cs, done + u + 1)
                        nc.gpsimd.tensor_tensor(kept[u % RING][:], marks[u % RING][:, 1, :], cand[u % RING][:],
                                                ALU.mult).then_inc(s_kept, 1)
                    for u in range(UNITS + 1):
                        if u < UNITS and u % 2:
                            mask(u)
                        if u:
                            keep(u - 1)
                steps(pool, body)

            @block.vector
            def _(dve):
                def start(k, parity):
                    dve.wait_ge(s_sort, SORT_INCS)
                    dve.sem_clear(s_sort)
                    wait(dve, s_bp, UNITS * (k - 1))
                    flat = idx[:].rearrange("p a b -> p (a b)")
                    nc.vector.tensor_scalar(hi[:].bitcast(U16), flat, 4, None,
                                            ALU.logical_shift_right).then_inc(s_idx, 1)
                    nc.vector.tensor_scalar(lo[:].bitcast(U16), flat, LO - 1, None,
                                            ALU.bitwise_and).then_inc(s_idx, 1)
                    nc.vector.tensor_scalar(nmax[:], w[1 - parity][:, :, 0], -1.0, None, ALU.mult)\
                        .then_inc(s_nmax, 1)

                def normalise(k, p):
                    dve.wait_ge(s_exp, k)
                    nc.vector.reciprocal(rtotal[:], total[:]).then_inc(s_rt, 1)
                    dve.wait_ge(s_rt, k)
                    nc.vector.tensor_tensor(w[p][:], w[p][:], rtotal[:].unsqueeze(2).to_broadcast([128, E, K]),
                                            ALU.mult).then_inc(s_wt, 1)

                def weigh(k, p, c):
                    dve.wait_ge(s_wt, k)
                    dve.wait_ge(s_acc, UNITS * (k - 1) + GROUPS * (c + 1))
                    flat = w[p][:].rearrange("p a b -> p (a b)")[:, c * WIDE:(c + 1) * WIDE]
                    nc.vector.tensor_tensor(flat, acc[:, :], flat, ALU.mult).then_inc(s_gx, 1)

                def activate(k, b):
                    dve.wait_ge(s_si, block_count(k, b))
                    wait(dve, s_dn, block_count(k, b) - 2)
                    nc.vector.tensor_tensor(act_s[b % 2][:], silu[:], p_h[0:HALF, 256:512],
                                            ALU.mult).then_inc(s_a, 1)

                def norm_moments(k):
                    dve.wait_ge(s_dn, BLOCKS * (k - 1))
                    nc.vector.bn_stats(stats[:], p_y[:, 0:D]).then_inc(s_st, 1)
                    dve.wait_ge(s_st, k - 1)
                    dve.sem_inc(s_held_v, 1)
                    nc.vector.bn_aggr(mv[:], stats[:]).then_inc(s_mv, 1)

                def norm_reciprocal(k):
                    dve.wait_ge(s_sd, k - 1)
                    nc.vector.reciprocal(rstd[:], sd[:]).then_inc(s_rs, 1)

                def norm_apply(k):
                    dve.wait_ge(s_rs, k - 1)
                    nc.vector.tensor_scalar(yn[:], p_y[:, 0:D], mv[:, 0:1], rstd[:, 0:1], ALU.subtract,
                                            ALU.mult).then_inc(s_yn, 1)

                def residual(k):
                    dve.wait_ge(s_h1, 16 * (k - 1))
                    wait(dve, s_out, 16 * (k - 2))
                    dve.wait_ge(s_op, k - 1)
                    nc.vector.tensor_tensor(res[:], p_misc[:, 0:D], h1t[:], ALU.add).then_inc(s_o, 1)

                def sort_round(parity, pair, r):
                    incs = 4 * (ROUNDS * pair + r)
                    feats = [g[parity][:, 2 * pair + i, :] for i in range(2)]
                    tops = [w[parity][:, 2 * pair + i, 8 * r:8 * r + 8] for i in range(2)]
                    for i in range(2):
                        if r:
                            dve.wait_ge(s_sort, incs - 1 + i)
                        nc.vector.max(tops[i], feats[i]).then_inc(s_sort, 1)
                    for i in range(2):
                        dve.wait_ge(s_sort, incs + 1 + i)
                        op = nc.vector.max_index(idx[:, 2 * pair + i, 8 * r:8 * r + 8], tops[i], feats[i])
                        if r == ROUNDS - 1:
                            op.then_inc(s_sort, 1)
                    for i in range(2):
                        if r < ROUNDS - 1:
                            nc.vector.match_replace(feats[i], tops[i], feats[i], LOWEST).then_inc(s_sort, 1)

                def body(k, parity):
                    p = 1 - parity
                    if gathers(k):
                        start(k, parity)
                    if sorts(k):
                        wait(dve, s_tp, E // BATCH * (k - 2) + 2)
                        dve.wait_ge(s_g, GATES * (k + 1))
                        nc.vector.tensor_copy(carrier[:], eps[:])
                    for step in range(ROUNDS * E // 2):
                        if sorts(k):
                            if step == ROUNDS * E // 4:
                                wait(dve, s_tp, E // BATCH * (k - 1))
                                nc.vector.tensor_copy(carrier[:], eps[:])
                            sort_round(parity, step // ROUNDS, step % ROUNDS)
                        if gathers(k):
                            if step == NORMALISE_STEP:
                                normalise(k, p)
                            for c in range(PARTS):
                                if step == WEIGH_STEPS[c]:
                                    weigh(k, p, c)
                        for b in range(BLOCKS):
                            if step == sort_step(BLOCK_ROUNDS[b]) and b in blocks_at(k, BLOCK_ROUNDS[b]):
                                activate(k, b)
                        if finishes(k):
                            if step == sort_step(SQRT_ROUND):
                                norm_moments(k)
                            if step == sort_step(SQRT_ROUND) + 4:
                                norm_reciprocal(k)
                                norm_apply(k)
                            if step == sort_step(MLP2_ROUND + 1):
                                residual(k)
                steps(dve, body)


def build(nc, t, out):
    h1_dram = nc.dram_tensor("h1_scratch", [PADDED, D], F32, kind="Internal").ap()
    x2_dram = nc.dram_tensor("x2_scratch", [PADDED, D], F32, kind="Internal").ap()
    parts_dram = nc.dram_tensor("parts_scratch", [SPLIT, PADDED, D], BF16, kind="Internal").ap()
    phase_a(nc, t, h1_dram, x2_dram, parts_dram)
    phase_b(nc, t, h1_dram, x2_dram, parts_dram, out)


def kernel(**inputs):
    import ml_dtypes
    import numpy as np
    import concourse.bacc as bacc
    from concourse.bass_utils import run_bass_kernel_spmd

    a = {n.replace("L0_", "").replace("ffn_", "").replace("attn_", ""): np.asarray(v) for n, v in inputs.items()}

    def chunked(m, p=HALF):
        return m.reshape(-1, p, m.shape[-1]).transpose(1, 0, 2)

    x = a["x"].reshape(IMAGES, CHANNELS, SIDE, PATCH, SIDE, PATCH).transpose(0, 1, 3, 5, 2, 4)
    x = x.reshape(IMAGES, PC, 128, SIDE * SIDE).transpose(0, 2, 1, 3)
    patches = np.zeros((IMAGES, 128, PC, TOKENS), x.dtype)
    patches[..., 1:] = x
    base = np.zeros((2 * CHUNK[0], D), x.dtype)
    base[:] = a["tok_b_lin"]
    base[0] = a["tok_cls_token"][0]
    wkv = np.zeros((2, HALF + 1, 2 * D), x.dtype)
    wkv[:, :HALF] = np.concatenate([a["Wk"].T, a["Wv"].T], axis=1).reshape(2, HALF, 2 * D)
    wkv[1, HALF] = np.concatenate([a["bk"], a["bv"]])
    tok = np.arange(128)
    pick = (tok[:, None] == np.repeat(tok, LO)[None, :]).reshape(128, GROUPS, GROUP * LO)
    gather = (np.arange(2 * 128 - GROUP)[None, :] - (128 - GROUP)) == (np.arange(GROUP * LO) // LO)[:, None]
    t = {
        "patches": patches,
        "w_lin": a["tok_W_lin"].T,
        "base": base.reshape(2, CHUNK[0], D),
        "wq": a["Wq"].T,
        "bq": a["bq"].reshape(2, HALF).T,
        "wkv": wkv,
        "ident": np.eye(128, dtype=np.float32),
        "pos_w": chunked(a["pos_w"]).reshape(HALF, 2 * D),
        "posT": chunked(a["posembed"].T).reshape(HALF, 2 * E),
        "pos_b": a["pos_b"][None],
        "gate_w": chunked(a["gate_w"]).reshape(HALF, 2 * D),
        "gate_b": a["gate_b"][None],
        "w_gu": np.concatenate([a["eg_w"], a["eu_w"]], axis=2).transpose(1, 0, 2),
        "w_dn": a["ed_w"].reshape(E, 2, HALF, D).transpose(2, 0, 1, 3),
        "ws_gu": chunked(np.concatenate([a["sg_w"], a["su_w"]], axis=1)),
        "ws_dn": a["sd_w"].reshape(SHARED, 2, HALF, D).transpose(2, 0, 1, 3),
        "m1": chunked(a["m1_w"]),
        "m2": chunked(a["m2_w"]),
        "m2b": a["m2_b"][None],
        "cols": np.concatenate([a[n].reshape(2, HALF) for n in ("ln_g", "ln_b", "m1_b")]).T,
        "pick": pick.astype(ml_dtypes.bfloat16),
        "gather": gather.astype(np.float32),
        "minus_slot": -(tok % LO).astype(np.float32)[:, None],
    }
    nc = bacc.Bacc("TRN2", target_bir_lowering=False, num_devices=1)
    arrays, aps = {}, {}
    for name, value in t.items():
        value = np.ascontiguousarray(value)
        arrays[f"in_{name}"] = value
        aps[name] = nc.dram_tensor(f"in_{name}", value.shape, mybir.dt.from_np(value.dtype),
                                   kind="ExternalInput").ap()
    out = nc.dram_tensor("out_rows", [TILES * 128, D], F32, kind="ExternalOutput").ap()
    build(nc, aps, out)
    result = run_bass_kernel_spmd(nc, [arrays], core_ids=[0]).results[0]["out_rows"]
    return result[:ROWS].reshape(IMAGES, TOKENS, D)
```
